# Optimizing a Trainium2 kernel written in Bass

```python
import numpy as np
import jax
import jax.numpy as jnp

def _softmax(x, axis=-1):
    return jax.nn.softmax(x, axis=axis)

def _gelu(x):
    return jax.nn.gelu(x, approximate=True)

def _silu(x):
    return jax.nn.silu(x)

def _sigmoid(x):
    return jax.nn.sigmoid(x)

def _layernorm(x, axis=-1, eps=1e-05):
    m = jnp.mean(x, axis=axis, keepdims=True)
    v = jnp.var(x, axis=axis, keepdims=True)
    return (x - m) / jnp.sqrt(v + eps)

def _scatter_add(tgt, idx, src, axis=0):
    return tgt.at[idx].add(src)

def _segment_sum(src, seg, n):
    return jax.ops.segment_sum(src, seg, n)
kernel_name = 'mk_prb_d1_jaxref_r8_c2dca7'

def setup_inputs(seed: int=0):
    np.random.seed(seed)
    _w = jnp.asarray

    def _L0_attn_setup():
        import math
        import jax, jax.numpy as jnp
        import numpy as np
        B, S, D, H = (1, 256, 256, 16)
        HD = D // H
        SCALE = HD ** (-0.5)
        EPS = 1e-05

        def _layernorm(y, w, b):
            mu = jnp.mean(y, -1, keepdims=True)
            var = jnp.mean((y - mu) ** 2, -1, keepdims=True)
            return (y - mu) * jax.lax.rsqrt(var + EPS) * w + b
        key = jax.random.key(seed)
        ks = jax.random.split(key, 8)
        std = D ** (-0.5)
        return {'x': jax.random.normal(ks[0], (B, S, D), jnp.float32), 'wq': jax.random.normal(ks[1], (D, D), jnp.float32) * std, 'wk': jax.random.normal(ks[2], (D, D), jnp.float32) * std, 'wv': jax.random.normal(ks[3], (D, D), jnp.float32) * std, 'wg': jax.random.normal(ks[4], (D, D), jnp.float32) * std, 'wo': jax.random.normal(ks[5], (D, D), jnp.float32) * std, 'ln_w': jnp.ones((D,), jnp.float32), 'ln_b': jnp.zeros((D,), jnp.float32)}
    _L0_attn_in = _L0_attn_setup()

    def _L0_ffn_setup():
        import jax, jax.numpy as jnp
        import numpy as np
        B, S, H = (1, 64, 256)
        I = 192
        E = 32
        K = 4
        SCALE = 1.8
        key = jax.random.key(seed)
        ks = jax.random.split(key, 9)
        init = lambda k, shape: jax.random.normal(k, shape, jnp.float32) * (1.0 / np.sqrt(shape[-1]))
        return {'x': jax.random.normal(ks[0], (B, S, H), jnp.float32), 'router_w': init(ks[1], (E, H)), 'router_b': jnp.zeros((E,), jnp.float32), 'gate_w': init(ks[2], (E, I, H)), 'up_w': init(ks[3], (E, I, H)), 'down_w': init(ks[4], (E, H, I)), 'shared_gate_w': init(ks[5], (I, H)), 'shared_up_w': init(ks[6], (I, H)), 'shared_down_w': init(ks[7], (H, I))}
    _L0_ffn_in = _L0_ffn_setup()
    _d = {'L0_attn_x': _L0_attn_in['x'], 'L0_attn_wq': _L0_attn_in['wq'], 'L0_attn_wk': _L0_attn_in['wk'], 'L0_attn_wv': _L0_attn_in['wv'], 'L0_attn_wg': _L0_attn_in['wg'], 'L0_attn_wo': _L0_attn_in['wo'], 'L0_attn_ln_w': _L0_attn_in['ln_w'], 'L0_attn_ln_b': _L0_attn_in['ln_b'], 'L0_ffn_router_w': _L0_ffn_in['router_w'], 'L0_ffn_router_b': _L0_ffn_in['router_b'], 'L0_ffn_gate_w': _L0_ffn_in['gate_w'], 'L0_ffn_up_w': _L0_ffn_in['up_w'], 'L0_ffn_down_w': _L0_ffn_in['down_w'], 'L0_ffn_shared_gate_w': _L0_ffn_in['shared_gate_w'], 'L0_ffn_shared_up_w': _L0_ffn_in['shared_up_w'], 'L0_ffn_shared_down_w': _L0_ffn_in['shared_down_w']}
    _x0 = _d['L0_attn_x']
    _d['L0_attn_x'] = jax.random.normal(jax.random.fold_in(jax.random.key(seed), 1), (2, 512, 256), dtype=_x0.dtype)
    del _x0
    return _d

def reference(L0_attn_x, L0_attn_wq, L0_attn_wk, L0_attn_wv, L0_attn_wg, L0_attn_wo, L0_attn_ln_w, L0_attn_ln_b, L0_ffn_router_w, L0_ffn_router_b, L0_ffn_gate_w, L0_ffn_up_w, L0_ffn_down_w, L0_ffn_shared_gate_w, L0_ffn_shared_up_w, L0_ffn_shared_down_w):

    def _L0_attn_ref(x, wq, wk, wv, wg, wo, ln_w, ln_b):
        import math
        import jax, jax.numpy as jnp
        import numpy as np
        B, S, D, H = (1, 256, 256, 16)
        HD = D // H
        SCALE = HD ** (-0.5)
        EPS = 1e-05

        def _layernorm(y, w, b):
            mu = jnp.mean(y, -1, keepdims=True)
            var = jnp.mean((y - mu) ** 2, -1, keepdims=True)
            return (y - mu) * jax.lax.rsqrt(var + EPS) * w + b
        bsz, seq_len, dim = x.shape

        def proj(w):
            return (x @ w.T).reshape(bsz, seq_len, H, HD).transpose(0, 2, 1, 3)
        q, k, v = (proj(wq), proj(wk), proj(wv))
        attn = jnp.einsum('bhid,bhjd->bhij', q, k) * SCALE
        gammas = 1.0 - jnp.exp(jnp.linspace(math.log(1 / 32), math.log(1 / 64), H)).astype(x.dtype)
        dist = jnp.arange(seq_len)[:, None] - jnp.arange(seq_len)[None, :]
        decay = gammas[:, None, None] ** jnp.abs(dist)[None]
        causal = (dist >= 0).astype(x.dtype)[None]
        scores = attn * (decay * causal)[None]
        y = jnp.einsum('bhij,bhjd->bhid', scores, v)
        y = y.transpose(0, 2, 1, 3).reshape(bsz, seq_len, dim)
        y = _layernorm(y, ln_w, ln_b)
        g = jax.nn.silu(x @ wg.T)
        return y * g @ wo.T

    def _L0_ffn_ref(x, router_w, router_b, gate_w, up_w, down_w, shared_gate_w, shared_up_w, shared_down_w):
        import jax, jax.numpy as jnp
        import numpy as np
        B, S, H = (1, 64, 256)
        I = 192
        E = 32
        K = 4
        SCALE = 1.8
        b, s, h = x.shape
        xf = x.reshape(-1, h).astype(jnp.float32)
        logits = xf @ router_w.T + router_b
        top_vals, top_idx = jax.lax.top_k(logits, K)
        rw = jax.nn.softmax(top_vals, axis=-1) * SCALE
        combine = jnp.einsum('tke,tk->te', jax.nn.one_hot(top_idx, E, dtype=xf.dtype), rw)
        g = jax.nn.silu(jnp.einsum('th,eih->tei', xf, gate_w))
        u = jnp.einsum('th,eih->tei', xf, up_w)
        routed = jnp.einsum('tei,ehi,te->th', g * u, down_w, combine)
        sg = jax.nn.silu(xf @ shared_gate_w.T)
        su = xf @ shared_up_w.T
        shared = sg * su @ shared_down_w.T
        return (routed + shared).reshape(b, s, h)
    x = L0_attn_x
    xn = _layernorm(x, axis=-1)
    x = x + _L0_attn_ref(xn, L0_attn_wq, L0_attn_wk, L0_attn_wv, L0_attn_wg, L0_attn_wo, L0_attn_ln_w, L0_attn_ln_b) + _L0_ffn_ref(xn, L0_ffn_router_w, L0_ffn_router_b, L0_ffn_gate_w, L0_ffn_up_w, L0_ffn_down_w, L0_ffn_shared_gate_w, L0_ffn_shared_up_w, L0_ffn_shared_down_w)
    return x

_drawn_inputs = setup_inputs


def setup_inputs(seed=0):
    import zlib

    import numpy as np

    out = dict(_drawn_inputs(seed))
    spreads = {'L0_attn_ln_w': (1.0, 0.2), 'L0_attn_ln_b': (0.0, 0.1), 'L0_ffn_router_b': (0.0, 0.1)}
    factors = {}
    for name, (base, spread) in spreads.items():
        noise = np.random.default_rng([zlib.crc32(name.encode()), seed]).standard_normal(out[name].shape)
        drawn = base * np.exp(spread * noise) if base else spread * noise
        out[name] = jnp.asarray(drawn.astype(out[name].dtype))
    for name, factor in factors.items():
        out[name] = (out[name] * factor).astype(out[name].dtype)
    return out
```

```python
from contextlib import ExitStack

import numpy as np

import concourse.bass as bass
from concourse import mybir

F32 = mybir.dt.float32
BF16 = mybir.dt.bfloat16
U32 = mybir.dt.uint32
I32 = mybir.dt.int32
ALU = mybir.AluOpType
ACT = mybir.ActivationFunctionType
AX_X = mybir.AxisListType.X

P = 128
BATCH, SEQ, D = 2, 512, 256
TOK = BATCH * SEQ
NT = TOK // P
CPB = SEQ // P
KT = D // P
H, HD = 16, 16
HG = P // HD
SCALE = HD ** -0.5
EPS = 1e-5
E, TOPK, I = 32, 4, 192
I2 = I - P
RSCALE = 1.8
RSQRT_MAGIC = 0x5F3759DF
EW = KT * 2 * I + D
ROWS = TOK * TOPK
NB = E + (ROWS - 1) // P
MAXB = TOK // P
NA = NT * TOPK
LATE = 15
RING = 4
Q_FIRST = 2
Q_LATE = (LATE + 1) // RING
Q_END = (NB - RING) // RING
T_RANK, T_INVERT, T_EXPERT = 1, 4, 5
LAG = 7

C_ID = 0
C_BM = C_ID + P
C_QD = C_BM + P
C_KD = C_QD + KT * P
C_GC = C_KD + H
C_PM = C_GC + KT
C_IO = C_PM + 2
C_PI = C_IO + P
C_FILL = C_PI + 1
C_TK = C_FILL + 1
C_LT = C_TK + NA
C_END = C_LT + P


def head_of_slot(s):
    r, par, g = s // 4, s // 2 % 2, s % 2
    return HG * g + 2 * r + par


def constants():
    gammas = (1.0 - np.exp(np.linspace(np.log(1 / 32), np.log(1 / 64), H)).astype(np.float32)).astype(np.float64)
    i = np.arange(P)
    c = np.zeros((P, C_END))
    c[:, C_ID:C_ID + P] = np.eye(P)
    c[:, C_BM:C_BM + P] = i[:, None] // HD == i[None, :] // HD
    for g in range(KT):
        row_gamma = gammas[HG * g + i // HD]
        c[:, C_QD + g * P:C_QD + (g + 1) * P] = SCALE * row_gamma[:, None] ** (i[None, :] + 1)
        c[:, C_GC + g] = row_gamma ** P
    c[:, C_KD:C_KD + H] = gammas[None, :] ** (P - 1 - i[:, None])
    for par in range(2):
        c[:, C_PM + par] = i // HD % 2 == par
    c[:, C_IO:C_IO + P] = i[None, :]
    c[:, C_PI] = i
    c[:, C_FILL] = ROWS + P + i
    for t in range(NT):
        for k in range(TOPK):
            c[:, C_TK + t * TOPK + k] = 1 + k * NT + t
    c[:, C_LT:C_LT + P] = i[:, None] < i[None, :]
    dist = i[None, :] - i[:, None]
    decay = np.zeros((P, H, P))
    for s in range(H):
        decay[:, s] = np.where(dist >= 0, SCALE * gammas[head_of_slot(s)] ** np.maximum(dist, 0), 0.0)
    return c.astype(np.float32), decay.reshape(P, H * P).astype(np.float32)


def build(nc, x, consts, decay, w_router, w_qkvg, w_out, w_sgu, w_sd1, w_sd2, lnwb, rbias, w_exp, w_exp2, xn_rows, y_rows, out):
    with ExitStack() as ctx:
        def sb(name, shape, dt=F32):
            return ctx.enter_context(nc.sbuf_tensor(name, shape, dt))

        def sem(name):
            return ctx.enter_context(nc.semaphore(name))

        w1 = sb("w1", [P, E * EW])
        w2 = sb("w2", [P, E * D])
        free1, free2 = [LATE * EW], [LATE * D]

        def early(*shape, dt=F32, of=w1, free=free1):
            n = int(np.prod(shape)) * mybir.dt.size(dt) // 4
            ap = of[:, free[0]:free[0] + n]
            free[0] += n
            assert free[0] <= of.shape[1]
            if dt != F32:
                ap = ap.bitcast(dt)
            if len(shape) == 2:
                ap = ap.rearrange("p (a b) -> p a b", a=shape[0])
            return ap

        x_sb = sb("x_sb", [P, NT, D])
        cst = sb("cst", [P, C_END])
        rw = sb("rw", [P, NA])
        codes = sb("codes", [P, NB, 2], U32)
        eid_row = sb("eid_row", [1, NB], I32)

        xn = early(NT, D)
        xnT = early(KT, TOK)
        dec = early(H * P)
        wqkvg = early(KT, 4 * D)
        st = early(H * P)
        wo = early(KT, D)
        wsgu = early(KT, 2 * I)
        wsd1 = early(D)
        lnw = early(D)
        lnb = early(D)
        wr = early(KT, E)
        rb = early(E)
        qk = early(2, 4 * P)
        qe = early(2, KT * P)
        qo = early(2, KT * P)
        qd = early(2, KT * P)
        v = early(2, D)
        wsd2 = sb("wsd2", [I2, D])
        stats = sb("stats", [P, NT, 6])
        mv = sb("mv", [P, NT, 2])
        rstd = sb("rstd", [P, NT])
        var = sb("var", [P, NT])
        newton = sb("newton", [P, NT])
        gate = early(3, D)
        ktok = sb("ktok", [P, D])
        state = sb("state", [P, KT * P])
        pmask = sb("pmask", [P, KT * P])
        ystats = sb("ystats", [P, 6])
        ymv = sb("ymv", [P, 2])
        yrstd = sb("yrstd", [P, 1])
        yn = sb("yn", [P, 2, D])
        z1 = early(D)
        z2 = early(D)
        z = early(2, D)
        sgs = sb("sgs", [P, I])
        hs = sb("hs", [P, 2, I])
        zT = sb("zT", [P, KT * P])
        hT1 = sb("hT1", [P, P])
        hT2 = sb("hT2", [I2, P])

        logits = sb("logits", [P, NT, E])
        top = sb("top", [P, NT, 8])
        topi = sb("topi", [P, NT, 8], U32)
        topf = sb("topf", [P, NT, TOPK])
        ex = sb("ex", [P, NT, TOPK])
        exs = sb("exs", [P, NT])
        chosen = sb("chosen", [P, NA, E], BF16)
        mask = sb("mask", [P, NT, E], BF16)
        lt_bf = sb("lt_bf", [P, P], BF16)
        ones_bf = sb("ones_bf", [P, P], BF16)
        ranks = sb("ranks", [P, NT, E])
        counts = sb("counts", [P, E])
        over = sb("over", [P, E, MAXB - 1], BF16)
        nblk = sb("nblk", [P, E])
        ends = sb("ends", [P, E])
        ones_e = sb("ones_e", [P, E])
        base = sb("base", [P, E])
        slot_k = sb("slot_k", [P, NA])
        slot_i = sb("slot_i", [P, NA], U32)
        blk_i = sb("blk_i", [P, NA], U32)
        pos_i = sb("pos_i", [P, NA], U32)
        blk_f = sb("blk_f", [P, NA])
        pos_f = sb("pos_f", [P, NA])
        prod = early(NA, E, of=w2, free=free2)
        pos_hot = early(NA, P, dt=BF16, of=w2, free=free2)
        blk_hot = early(NA, NB, dt=BF16, of=w2, free=free2)
        loop_mem = sb("loop_mem", [P, RING * D + 2 * KT * P + 2 * I + 2 * NB])
        blk_code = loop_mem[:, 0:NA * NB].bitcast(BF16).rearrange("p (a b) -> p a b", a=NA)

        xg = sb("xg", [P, RING, D])
        xbT = sb("xbT", [P, 2, KT * P])
        eh = sb("eh", [P, 2, KT * P])
        gidx = sb("gidx", [P, RING], U32)
        sidx = sb("sidx", [P, RING], U32)
        ysb = loop_mem[:, 0:RING * D].rearrange("p (a b) -> p a b", a=RING)
        ehT = loop_mem[:, RING * D:RING * D + 2 * KT * P].rearrange("p (a b) -> p a b", a=2)
        sil = loop_mem[:, RING * D + 2 * KT * P:RING * D + 2 * KT * P + 2 * I].rearrange("p (a b) -> p a b", a=2)
        back = w1[:, 0:NA * D].rearrange("p (t k d) -> p t k d", t=NT, k=TOPK)
        inv = sb("inv", [P, 2 * NB])
        unused = sb("unused", [P, NB])
        code_f = sb("code_f", [P, NB])
        le = sb("le", [P, E])
        eid = sb("eid", [P, 1])

        bank = [ctx.enter_context(nc.psum_tensor(f"bank{i}", [P, 512], F32)) for i in range(8)]
        ps_tr, ps_qk, ps_vg, ps_sg, ps_s0, ps_s1, ps_y, ps_po = bank
        ps_s = [ps_s0, ps_s1]
        ps_xt, ps_gu, ps_eht, ps_dn = [ps_tr, ps_qk], [ps_vg, ps_sg], [ps_s0, ps_s1], [ps_y, ps_po]

        ident = cst[:, C_ID:C_ID + P]

        x_in = sem("x_in")
        c_in = sem("c_in")
        w_in = sem("w_in")
        wq_in = sem("wq_in")
        d_in = sem("d_in")
        dve_step = sem("dve_step")
        pool_seq = sem("pool_seq")
        xn_done = sem("xn_done")
        xnT_ps = sem("xnT_ps")
        xnT_sb = sem("xnT_sb")
        lg_ps = sem("lg_ps")
        lg_sb = sem("lg_sb")
        qk_ps = sem("qk_ps")
        qk_sb = sem("qk_sb")
        q_ready = sem("q_ready")
        vg_ps = sem("vg_ps")
        vg_sb = sem("vg_sb")
        sg_ps = sem("sg_ps")
        sgs_sb = sem("sgs_sb")
        hs_sb = sem("hs_sb")
        sc_ps = sem("sc_ps")
        sc_sb = sem("sc_sb")
        kt_ps = sem("kt_ps")
        kt_sb = sem("kt_sb")
        pr_ps = sem("pr_ps")
        st_sb = sem("st_sb")
        y_ps = sem("y_ps")
        yn_sb = sem("yn_sb")
        z_sb = sem("z_sb")
        trb_ps = sem("trb_ps")
        trb_sb = sem("trb_sb")
        o_ps = sem("o_ps")
        res_sb = sem("res_sb")
        out_done = sem("out_done")
        xn_out = sem("xn_out")
        we_in = sem("we_in")
        wl_in = sem("wl_in")
        pool_cst = sem("pool_cst")
        soft_in = sem("soft_in")
        soft_ex = sem("soft_ex")
        mask_sb = sem("mask_sb")
        rank_ps = sem("rank_ps")
        rank_sb = sem("rank_sb")
        hot_sb = sem("hot_sb")
        inv_ps = sem("inv_ps")
        inv_sb = sem("inv_sb")
        eid_ps = sem("eid_ps")
        eid_in = sem("eid_in")
        eid_sb = sem("eid_sb")
        gidx_sb = sem("gidx_sb")
        pool_go = sem("pool_go")
        tok_in = [sem(f"tok_in{i}") for i in range(RING)]
        xt_ps = sem("xt_ps")
        xt_sb = sem("xt_sb")
        gu_ps = sem("gu_ps")
        sil_sb = sem("sil_sb")
        eh_sb = sem("eh_sb")
        eht_ps = sem("eht_ps")
        eht_sb = sem("eht_sb")
        dn_ps = sem("dn_ps")
        ys_sb = sem("ys_sb")
        sent = [sem(f"sent{i}") for i in range(RING)]
        back_in = [sem(f"back_in{i}") for i in range(NT)]
        tot_sb = sem("tot_sb")

        block = ctx.enter_context(nc.Block())
        x_v = x.rearrange("b (t p) d -> p (b t) d", p=P)
        out_v = out.rearrange("b (t p) d -> p (b t) d", p=P)

        def states_before(t):
            return sum(1 for u in range(t) if u % CPB < CPB - 1)

        def need(eng, semaphore, value):
            if not isinstance(value, int) or value > 0:
                eng.wait_ge(semaphore, value)

        def expert_loop(eng, step, before_late=None):
            for i in range(RING * Q_FIRST):
                step(i // RING, i % RING, i)
            with eng.Fori(Q_FIRST, Q_LATE) as q:
                for u in range(RING):
                    step(q, u, None)
            if before_late:
                before_late()
            with eng.Fori(Q_LATE, Q_END) as q:
                for u in range(RING):
                    step(q, u, None)
            for i in range(RING * Q_END, NB + 3):
                step(i // RING, i % RING, i)

        def live(i, stage):
            return i is None or 0 <= i - stage < NB

        @block.sync
        def _(sp):
            for t in range(NT):
                sp.dma_start(x_sb[:, t, :], x_v[:, t, :]).then_inc(x_in, 16)
            sp.dma_start(dec[:, :], decay).then_inc(d_in, 16)
            for half in range(2):
                s = slice(half * NT // 2, (half + 1) * NT // 2)
                sp.wait_ge(xn_done, (half + 1) * NT // 2)
                sp.dma_start(xn_rows.rearrange("(t p) d -> p t d", p=P)[:, s, :], xn[:, s, :]).then_inc(xn_out, 16)
            for e in range(0, LATE, 5):
                sp.dma_start(w1[:, e * EW:(e + 5) * EW], w_exp[:, e * EW:(e + 5) * EW]).then_inc(we_in, 16)
            sp.dma_start(w2[0:I2, 0:LATE * D], w_exp2[:, 0:LATE * D]).then_inc(we_in, 16)
            sp.wait_ge(xn_out, 32)
            sp.wait_ge(res_sb, NT)
            late = list(range(LATE, E, 4)) + [E]
            for e, f in zip(late, late[1:]):
                sp.dma_start(w1[:, e * EW:f * EW], w_exp[:, e * EW:f * EW]).then_inc(wl_in, 16)
                if e == LATE:
                    sp.dma_start(w2[0:I2, LATE * D:E * D], w_exp2[:, LATE * D:E * D]).then_inc(wl_in, 16)
            for s in range(RING):
                sp.wait_ge(sent[s], 16 * ((NB - 1 - s) // RING + 1))
            y_v = y_rows.rearrange("(k t p) d -> t p k d", t=NT, p=P)
            for t in range(NT):
                sp.dma_start(back[:, t], y_v[t]).then_inc(back_in[t], 16)
            for t in range(NT):
                sp.wait_ge(tot_sb, t + 1)
                sp.dma_start(out_v[:, t, :], x_sb[:, t, :]).then_inc(out_done, 16)
            sp.wait_ge(out_done, 16 * NT)

        @block.scalar
        def _(act):
            act.dma_start(cst[:, :], consts).then_inc(c_in, 16)
            act.dma_start(wr[:, :, :], w_router).then_inc(c_in, 16)
            act.dma_start(rb[:, :], rbias.partition_broadcast(P)).then_inc(c_in, 16)
            act.dma_start(wqkvg[:, :, :], w_qkvg).then_inc(wq_in, 16)
            act.dma_start(wsgu[:, :, :], w_sgu).then_inc(w_in, 16)
            act.dma_start(wo[:, :, :], w_out).then_inc(w_in, 16)
            act.dma_start(wsd1[:, :], w_sd1).then_inc(w_in, 16)
            act.dma_start(wsd2[:, :], w_sd2).then_inc(w_in, 16)
            act.dma_start(lnw[:, :], lnwb[0].partition_broadcast(P)).then_inc(w_in, 16)
            act.dma_start(lnb[:, :], lnwb[1].partition_broadcast(P)).then_inc(w_in, 16)

            for u in range(NT // 2):
                act.wait_ge(xnT_ps, u + 1)
                nc.scalar.copy(xnT[:, :, 2 * u * P:2 * (u + 1) * P],
                               ps_s[u % 2][:, :].rearrange("p (g n) -> p g n", g=KT)).then_inc(xnT_sb, 1)

            def take_projections(t):
                act.wait_ge(qk_ps, t + 1)
                nc.scalar.copy(qk[:, t % 2, :], ps_qk[:, :]).then_inc(qk_sb, 1)
                act.wait_ge(vg_ps, t + 1)
                nc.scalar.copy(v[:, t % 2, :], ps_vg[:, 0:D]).then_inc(vg_sb, 1)
                nc.scalar.activation(gate[:, t % 3, :], ps_vg[:, D:2 * D], ACT.Silu).then_inc(vg_sb, 1)

            def take_shared_gate(t):
                act.wait_ge(sg_ps, t + 1)
                nc.scalar.activation(sgs[:, :], ps_sg[:, 0:I], ACT.Silu).then_inc(sgs_sb, 1)

            def take_transposed(t):
                act.wait_ge(trb_ps, t + 1)
                nc.scalar.copy(hT1[:, :], ps_tr[:, 0:P]).then_inc(trb_sb, 1)
                nc.scalar.copy(hT2[:, :], ps_tr[0:I2, P:2 * P]).then_inc(trb_sb, 1)
                nc.scalar.copy(zT[:, :], ps_tr[:, 2 * P:4 * P]).then_inc(trb_sb, 1)

            act.wait_ge(soft_in, 1)
            nc.scalar.activation(ex[:, :, :], ex[:, :, :], ACT.Exp).then_inc(soft_ex, 1)
            take_projections(0)
            take_shared_gate(0)
            for t in range(NT):
                if t + 1 < NT:
                    take_projections(t + 1)
                if t >= 1:
                    take_transposed(t - 1)
                if t + 1 < NT:
                    take_shared_gate(t + 1)
            take_transposed(NT - 1)

            def step(q, u, i):
                n = RING * q + u
                if live(i, 0):
                    need(act, xt_ps, n + 1)
                    need(act, gu_ps, n - 1)
                    nc.scalar.copy(xbT[:, u % 2, :], ps_xt[u % 2][:, 0:KT * P]).then_inc(xt_sb, 1)
                if live(i, 1):
                    need(act, gu_ps, n)
                    need(act, eh_sb, n - 2)
                    nc.scalar.activation(sil[:, (u - 1) % 2, :], ps_gu[(u - 1) % 2][:, 0:I], ACT.Silu).then_inc(sil_sb, 1)
                if live(i, 2):
                    need(act, eht_ps, n - 1)
                    need(act, dn_ps, n - 3)
                    nc.scalar.copy(ehT[:, u % 2, :], ps_eht[u % 2][:, 0:KT * P]).then_inc(eht_sb, 1)

            expert_loop(act, step)

        @block.gpsimd
        def _(pool):
            steps = [0]

            def step(ins):
                steps[0] += 1
                ins.then_inc(pool_seq, 1)
                pool.wait_ge(pool_seq, steps[0])

            def mask_queries(t):
                pool.wait_ge(qk_sb, t + 1)
                if t == 0:
                    pool.wait_ge(c_in, 48)
                q = qk[:, t % 2, 0:KT * P]
                nc.gpsimd.tensor_scalar(qe[:, t % 2, :], q, cst[:, C_PM:C_PM + 1], None, ALU.mult).then_inc(q_ready, 1)
                nc.gpsimd.tensor_scalar(qo[:, t % 2, :], q, cst[:, C_PM + 1:C_PM + 2], None, ALU.mult).then_inc(q_ready, 1)
                nc.gpsimd.tensor_tensor(qd[:, t % 2, :], q, cst[:, C_QD:C_QD + KT * P], ALU.mult).then_inc(q_ready, 1)

            def gate_output(t):
                pool.wait_ge(yn_sb, t + 1)
                if t == 0:
                    pool.wait_ge(w_in, 96)
                step(nc.gpsimd.tensor_tensor(z1[:, :], yn[:, t % 2, :], lnw[:, :], ALU.mult))
                step(nc.gpsimd.tensor_tensor(z2[:, :], z1[:, :], lnb[:, :], ALU.add))
                pool.wait_ge(vg_sb, 2 * (t + 1))
                nc.gpsimd.tensor_tensor(z[:, t % 2, :], z2[:, :], gate[:, t % 3, :], ALU.mult).then_inc(z_sb, 1)

            def pool_step(q, u, j):
                n = RING * q + u
                if live(j, 0):
                    need(pool, gidx_sb, n + 1)
                    pool.sem_inc(pool_go, 1)
                    need(pool, xt_ps, n - RING + 1)
                    pool.sem_inc(pool_go, 1)
                    nc.gpsimd.indirect_dma_start(
                        xg[:, u, :], None, xn_rows, bass.IndirectOffsetOnAxis(ap=gidx[:, u:u + 1], axis=0),
                    ).then_inc(tok_in[u], 16)
                if live(j, LAG):
                    w = (u - LAG) % RING
                    need(pool, ys_sb, n - LAG + 1)
                    pool.sem_inc(pool_go, 1)
                    nc.gpsimd.indirect_dma_start(
                        y_rows, bass.IndirectOffsetOnAxis(ap=sidx[:, w:w + 1], axis=0), ysb[:, w, :], None,
                        bounds_check=ROWS - 1, oob_is_err=False,
                    ).then_inc(sent[w], 16)

            pool.wait_ge(c_in, 48)
            nc.gpsimd.memset(ones_bf[:, :], 1.0)
            nc.gpsimd.memset(ones_e[:, :], 1.0)
            nc.gpsimd.memset(eh[:, :, :], 0.0)
            nc.gpsimd.tensor_copy(lt_bf[:, :], cst[:, C_LT:C_LT + P]).then_inc(pool_cst, 1)
            mask_queries(0)
            for t in range(NT):
                if t + 1 < NT:
                    mask_queries(t + 1)
                gate_output(t)
                if t == NT - 2:
                    pool.wait_ge(xn_out, 32)
                    for j in range(RING):
                        pool_step(0, j, j)
            for j in range(RING, Q_FIRST * RING):
                pool_step(j // RING, j % RING, j)
            with pool.Fori(Q_FIRST, NB // RING) as q:
                for u in range(RING):
                    pool_step(q, u, None)
            for j in range(RING * (NB // RING), NB + LAG):
                pool_step(j // RING, j % RING, j)

        @block.vector
        def _(dve):
            steps = [0]

            def step(ins):
                steps[0] += 1
                ins.then_inc(dve_step, 1)
                dve.wait_ge(dve_step, steps[0])

            def inverse_sqrt(y, variance, v, a):
                step(nc.vector.tensor_scalar(v, variance, EPS, None, ALU.add))
                step(nc.vector.tensor_scalar(a.bitcast(I32), v.bitcast(I32), 1, None, ALU.logical_shift_right))
                step(nc.vector.tensor_scalar(y.bitcast(I32), a.bitcast(I32), -1, RSQRT_MAGIC, ALU.mult, ALU.add))
                for _ in range(3):
                    step(nc.vector.tensor_tensor(a, y, y, ALU.mult))
                    step(nc.vector.tensor_tensor(a, a, v, ALU.mult))
                    step(nc.vector.tensor_scalar(a, a, -0.5, 1.5, ALU.mult, ALU.add))
                    step(nc.vector.tensor_tensor(y, y, a, ALU.mult))

            for half in range(2):
                tiles = range(half * NT // 2, (half + 1) * NT // 2)
                for t in tiles:
                    if t % (NT // 2) == 0:
                        dve.wait_ge(x_in, 16 * NT)
                    last = nc.vector.bn_stats(stats[:, t, :], x_sb[:, t, :])
                step(last)
                for t in tiles:
                    last = nc.vector.bn_aggr(mv[:, t, :], stats[:, t, :])
                step(last)
                s = slice(tiles[0], tiles[-1] + 1)
                inverse_sqrt(rstd[:, s], mv[:, s, 1], var[:, s], newton[:, s])
                for t in tiles:
                    nc.vector.tensor_scalar(xn[:, t, :], x_sb[:, t, :], mv[:, t, 0:1], rstd[:, t:t + 1],
                                            ALU.subtract, ALU.mult).then_inc(xn_done, 1)
            dve.wait_ge(lg_ps, NT)
            dve.wait_ge(c_in, 48)
            ins = nc.vector.tensor_tensor(logits[:, :, :], ps_y[:, 0:NT * E].rearrange("p (t e) -> p t e", t=NT),
                                          rb[:, :].unsqueeze(1).broadcast_to([P, NT, E]), ALU.add)
            step(ins)

            for t in range(NT):
                last = nc.vector.max(top[:, t, :], logits[:, t, :])
            step(last)
            for t in range(NT):
                last = nc.vector.max_index(topi[:, t, :], top[:, t, :], logits[:, t, :])
            step(last)
            nc.vector.tensor_tensor(ex[:, :, :], top[:, :, 0:TOPK], top[:, :, 0:1].broadcast_to([P, NT, TOPK]),
                                    ALU.subtract).then_inc(soft_in, 1)
            step(nc.vector.tensor_copy(topf[:, :, :], topi[:, :, 0:TOPK]))
            step(nc.vector.tensor_tensor(
                chosen[:, :, :], cst[:, C_IO:C_IO + E].unsqueeze(1).broadcast_to([P, NA, E]),
                topf[:, :, :].rearrange("p t k -> p (t k)").unsqueeze(2).broadcast_to([P, NA, E]), ALU.is_equal))
            with nc.allow_low_precision(reason="the sums are 0 or 1"):
                nc.vector.tensor_reduce(mask[:, :, :], chosen[:, :, :].rearrange("p (t k) e -> p t e k", k=TOPK),
                                        AX_X, ALU.add).then_inc(mask_sb, 1)
            dve.wait_ge(soft_ex, 1)
            step(nc.vector.reduce_sum(exs[:, :], ex[:, :, :], AX_X))
            step(nc.vector.reciprocal(exs[:, :], exs[:, :]))
            nc.vector.scalar_tensor_tensor(rw[:, :].rearrange("p (t k) -> p t k", k=TOPK), ex[:, :, :], RSCALE,
                                           exs[:, :].unsqueeze(2).broadcast_to([P, NT, TOPK]), ALU.mult, ALU.mult)

            def take_ranks():
                dve.wait_ge(rank_ps, 1)
                nc.vector.tensor_copy(ranks[:, :, :], ps_y[:, D:2 * D].rearrange("p (t e) -> p t e", t=NT))
                nc.vector.tensor_scalar(counts[:, :], ps_y[:, 0:E], 1.0 / P, None, ALU.mult).then_inc(rank_sb, 1)

            def assign_slots():
                dve.wait_ge(rank_sb, 1)
                step(nc.vector.tensor_tensor(over[:, :, :], counts[:, :].unsqueeze(2).broadcast_to([P, E, MAXB - 1]),
                                             cst[:, C_IO + 1:C_IO + MAXB].unsqueeze(1).broadcast_to([P, E, MAXB - 1]),
                                             ALU.is_gt))
                step(nc.vector.reduce_sum(nblk[:, :], over[:, :, :], AX_X))
                step(nc.vector.tensor_scalar(nblk[:, :], nblk[:, :], 1.0, None, ALU.add))
                dve.wait_ge(pool_cst, 1)
                step(nc.vector.tensor_tensor_scan(ends[:, :], ones_e[:, :], nblk[:, :], 0.0, ALU.mult, ALU.add))
                step(nc.vector.tensor_tensor(base[:, :], ends[:, :], nblk[:, :], ALU.subtract))
                step(nc.vector.tensor_scalar(base[:, :], base[:, :], float(P), None, ALU.mult))
                step(nc.vector.tensor_tensor(ranks[:, :, :], ranks[:, :, :],
                                             base[:, :].unsqueeze(1).broadcast_to([P, NT, E]), ALU.add))
                step(nc.vector.tensor_tensor(
                    prod[:, :, :].rearrange("p (t k) e -> p t k e", k=TOPK),
                    chosen[:, :, :].rearrange("p (t k) e -> p t k e", k=TOPK),
                    ranks[:, :, :].unsqueeze(2).broadcast_to([P, NT, TOPK, E]), ALU.mult))
                step(nc.vector.reduce_sum(slot_k[:, :], prod[:, :, :], AX_X))
                step(nc.vector.tensor_copy(slot_i[:, :], slot_k[:, :]))
                step(nc.vector.tensor_scalar(blk_i[:, :], slot_i[:, :], P.bit_length() - 1, None,
                                             ALU.logical_shift_right))
                step(nc.vector.tensor_scalar(pos_i[:, :], slot_i[:, :], P - 1, None, ALU.bitwise_and))
                nc.vector.tensor_copy(blk_f[:, :], blk_i[:, :])
                step(nc.vector.tensor_copy(pos_f[:, :], pos_i[:, :]))

            def one_hot_positions():
                nc.vector.tensor_tensor(pos_hot[:, :, :], cst[:, C_IO:C_IO + P].unsqueeze(1).broadcast_to([P, NA, P]),
                                        pos_f[:, :].unsqueeze(2).broadcast_to([P, NA, P]), ALU.is_equal)

            def one_hot_blocks():
                step(nc.vector.tensor_tensor(blk_hot[:, :, :], cst[:, C_IO:C_IO + NB].unsqueeze(1).broadcast_to([P, NA, NB]),
                                             blk_f[:, :].unsqueeze(2).broadcast_to([P, NA, NB]), ALU.is_equal))
                nc.vector.tensor_tensor(blk_code[:, :, 0:NB], blk_hot[:, :, :],
                                        cst[:, C_TK:C_TK + NA].unsqueeze(2).broadcast_to([P, NA, NB]), ALU.mult)
                nc.vector.tensor_scalar(blk_code[:, :, NB:2 * NB], blk_hot[:, :, :], cst[:, C_PI:C_PI + 1], None,
                                        ALU.mult).then_inc(hot_sb, 1)

            def take_inverse():
                dve.wait_ge(inv_ps, 1)
                nc.vector.tensor_copy(inv[:, :], ps_y[:, D:D + 2 * NB]).then_inc(inv_sb, 1)

            def make_codes():
                dve.wait_ge(inv_sb, 1)
                nc.vector.tensor_scalar(unused[:, :], inv[:, 0:NB], 0.0, cst[:, C_FILL:C_FILL + 1],
                                        ALU.is_equal, ALU.mult)
                step(nc.vector.tensor_scalar(code_f[:, :], inv[:, 0:NB], float(P), float(-P), ALU.mult, ALU.add))
                step(nc.vector.tensor_tensor(code_f[:, :], code_f[:, :], unused[:, :], ALU.add))
                step(nc.vector.tensor_tensor(codes[:, :, 1], code_f[:, :], inv[:, NB:2 * NB], ALU.add))
                step(nc.vector.tensor_scalar(codes[:, :, 0], codes[:, :, 1], TOK - 1, None, ALU.bitwise_and))
                nc.vector.tensor_copy(gidx[:, :], codes[:, 0:RING, 0]).then_inc(gidx_sb, RING)
                step(nc.vector.tensor_scalar(le[:, :], ends[:, :], cst[:, C_PI:C_PI + 1], None, ALU.is_le))
                step(nc.vector.reduce_sum(eid[:, :], le[:, :], AX_X))
                nc.vector.tensor_scalar(eid[:, :], eid[:, :], float(E - 1), None, ALU.min).then_inc(eid_in, 1)

            def take_block_experts():
                dve.wait_ge(eid_ps, 1)
                nc.vector.tensor_copy(eid_row[:, :], ps_y[0:1, D:D + NB]).then_inc(eid_sb, 1)

            def decay_scores(t, r):
                dve.wait_ge(sc_ps, 4 * t + r + 1)
                if t == 0 and r == 0:
                    dve.wait_ge(d_in, 16)
                nc.vector.tensor_tensor(st[:, 4 * r * P:4 * (r + 1) * P], ps_s[r % 2][:, :],
                                        dec[:, 4 * r * P:4 * (r + 1) * P], ALU.mult).then_inc(sc_sb, 1)

            def decay_keys(t):
                dve.wait_ge(kt_ps, states_before(t) + 1)
                nc.vector.tensor_tensor(ktok[:, :].rearrange("p (h d) -> p h d", h=H),
                                        ps_tr[:, 0:D].rearrange("p (h d) -> p h d", h=H),
                                        cst[:, C_KD:C_KD + H].unsqueeze(2).broadcast_to([P, H, HD]),
                                        ALU.mult).then_inc(kt_sb, 1)

            def update_state(t):
                dve.wait_ge(pr_ps, states_before(t) + 1)
                first = t % CPB == 0
                to = state if first else pmask
                ins = nc.vector.tensor_tensor(to[:, :].rearrange("p (g n) -> p g n", g=KT),
                                              ps_po[:, 0:KT * P].rearrange("p (g n) -> p g n", g=KT),
                                              cst[:, C_BM:C_BM + P].unsqueeze(1).broadcast_to([P, KT, P]), ALU.mult)
                if first:
                    ins.then_inc(st_sb, 1)
                    return
                step(ins)
                for g in range(KT):
                    s = slice(g * P, (g + 1) * P)
                    last = nc.vector.scalar_tensor_tensor(state[:, s], state[:, s], cst[:, C_GC + g:C_GC + g + 1],
                                                          pmask[:, s], ALU.mult, ALU.add)
                last.then_inc(st_sb, 1)

            def shared_hidden(t):
                dve.wait_ge(sgs_sb, t + 1)
                nc.vector.tensor_tensor(hs[:, t % 2, :], sgs[:, :], ps_sg[:, I:2 * I], ALU.mult).then_inc(hs_sb, 1)

            def add_residual(t):
                dve.wait_ge(o_ps, t + 1)
                nc.vector.tensor_tensor(x_sb[:, t, :], x_sb[:, t, :], ps_po[:, D:2 * D], ALU.add).then_inc(res_sb, 1)

            def normalise_output(t):
                dve.wait_ge(y_ps, t + 1)
                step(nc.vector.bn_stats(ystats[:, :], ps_y[:, 0:D]))
                step(nc.vector.bn_aggr(ymv[:, :], ystats[:, :]))
                inverse_sqrt(yrstd[:, :], ymv[:, 1:2], var[:, 0:1], newton[:, 0:1])
                if t >= 2:
                    dve.wait_ge(z_sb, t - 1)
                nc.vector.tensor_scalar(yn[:, t % 2, :], ps_y[:, 0:D], ymv[:, 0:1], yrstd[:, :],
                                        ALU.subtract, ALU.mult).then_inc(yn_sb, 1)

            shared_hidden(0)
            for t in range(NT):
                decay_scores(t, 0)
                decay_scores(t, 1)
                if t % CPB < CPB - 1:
                    decay_keys(t)
                decay_scores(t, 2)
                if t == T_RANK:
                    take_ranks()
                if t == T_INVERT:
                    take_inverse()
                if t == T_EXPERT:
                    take_block_experts()
                if t % CPB < CPB - 1:
                    update_state(t)
                decay_scores(t, 3)
                if t + 1 < NT:
                    shared_hidden(t + 1)
                normalise_output(t)
                if t >= 1:
                    add_residual(t - 1)
                if t == T_RANK:
                    assign_slots()
                if t == T_RANK + 1:
                    one_hot_positions()
                if t == T_RANK + 2:
                    one_hot_blocks()
                if t == T_INVERT:
                    make_codes()
            add_residual(NT - 1)

            def expert_step(q, u, i):
                n = RING * q + u
                if live(i, -RING):
                    need(dve, tok_in[u], 16 * (q + 1))
                    nc.vector.tensor_copy(gidx[:, u:u + 1], codes[:, bass.ds(n + RING, 1), 0]).then_inc(gidx_sb, 1)
                if live(i, 1):
                    need(dve, sil_sb, n)
                    need(dve, eht_ps, n - 2)
                    nc.vector.tensor_tensor(eh[:, (u - 1) % 2, 0:I], sil[:, (u - 1) % 2, :],
                                            ps_gu[(u - 1) % 2][:, I:2 * I], ALU.mult).then_inc(eh_sb, 1)
                if live(i, 3):
                    w = (u - 3) % RING
                    need(dve, sent[w], 16 * (q + (u - 3) // RING))
                    nc.vector.tensor_copy(sidx[:, w:w + 1], codes[:, bass.ds(n - 3, 1), 1])
                    need(dve, dn_ps, n - 2)
                    nc.vector.tensor_copy(ysb[:, w, :], ps_dn[(u - 3) % 2][:, 0:D]).then_inc(ys_sb, 1)

            expert_loop(dve, expert_step)

            for t in range(NT):
                dve.wait_ge(back_in[t], 16)
                for k in range(TOPK):
                    a = t * TOPK + k
                    ins = nc.vector.scalar_tensor_tensor(x_sb[:, t, :], back[:, t, k, :], rw[:, a:a + 1], x_sb[:, t, :],
                                                         ALU.mult, ALU.add)
                    if k < TOPK - 1:
                        step(ins)
                ins.then_inc(tot_sb, 1)

        @block.tensor
        def _(pe):
            pe.wait_ge(c_in, 48)
            for u in range(NT // 2):
                pe.wait_ge(xn_done, 2 * u + 2)
                if u >= 2:
                    pe.wait_ge(xnT_sb, u - 1)
                for g in range(KT):
                    for j in range(2):
                        o = (2 * g + j) * P
                        last = nc.tensor.transpose(ps_s[u % 2][:, o:o + P], xn[:, 2 * u + j, g * P:(g + 1) * P], ident)
                last.then_inc(xnT_ps, 1)
            for t in range(NT):
                if t % 2 == 0:
                    pe.wait_ge(xnT_sb, t // 2 + 1)
                for g in range(KT):
                    last = nc.tensor.matmul(ps_y[:, t * E:(t + 1) * E], xnT[:, g, t * P:(t + 1) * P], wr[:, g, :],
                                            start=(g == 0), stop=(g == KT - 1))
                last.then_inc(lg_ps, 1)

            def route_ranks():
                pe.wait_ge(pool_cst, 1)
                pe.wait_ge(mask_sb, 1)
                nc.tensor.matmul(ps_y[:, D:2 * D], lt_bf[:, :], mask[:, :, :].rearrange("p t e -> p (t e)"),
                                 start=True, stop=False, skip_group_check=True)
                for t in range(NT - 1):
                    after = NT - 1 - t
                    nc.tensor.matmul(ps_y[:, D + (t + 1) * E:2 * D].rearrange("p (t e) -> p t e", e=E), ones_bf[:, :],
                                     mask[:, t:t + 1, :].broadcast_to([P, after, E]),
                                     start=False, stop=True, skip_group_check=True)
                for t in range(NT):
                    last = nc.tensor.matmul(ps_y[:, 0:E], ones_bf[:, :], mask[:, t, :],
                                            start=False, stop=(t == NT - 1), skip_group_check=True)
                last.then_inc(rank_ps, 1)

            def route_inverse():
                pe.wait_ge(hot_sb, 1)
                for a in range(NA):
                    last = nc.tensor.matmul(ps_y[:, D:D + 2 * NB], pos_hot[:, a, :], blk_code[:, a, :],
                                            start=(a == 0), stop=(a == NA - 1))
                last.then_inc(inv_ps, 1)

            def tokens(g, t):
                return xnT[:, g, t * P:(t + 1) * P]

            def project_qk(t):
                if t >= 1:
                    pe.wait_ge(qk_sb, t)
                for m in range(2 * KT):
                    for g in range(KT):
                        last = nc.tensor.matmul(ps_qk[:, m * P:(m + 1) * P], wqkvg[:, g, m * P:(m + 1) * P],
                                                tokens(g, t), start=(g == 0), stop=(g == KT - 1))
                last.then_inc(qk_ps, 1)

            def project_vg(t):
                if t >= 1:
                    pe.wait_ge(vg_sb, 2 * t)
                for g in range(KT):
                    last = nc.tensor.matmul(ps_vg[:, :], tokens(g, t), wqkvg[:, g, 2 * D:4 * D],
                                            start=(g == 0), stop=(g == KT - 1))
                last.then_inc(vg_ps, 1)

            def project_shared(t):
                if t == 0:
                    pe.wait_ge(w_in, 96)
                else:
                    pe.wait_ge(hs_sb, t)
                for g in range(KT):
                    last = nc.tensor.matmul(ps_sg[:, 0:2 * I], tokens(g, t), wsgu[:, g, :],
                                            start=(g == 0), stop=(g == KT - 1))
                last.then_inc(sg_ps, 1)

            def scores(t, r):
                n = 4 * t + r
                if r == 0:
                    pe.wait_ge(q_ready, 3 * (t + 1))
                if n >= 2:
                    pe.wait_ge(sc_sb, n - 1)
                rows = slice(32 * r, 32 * (r + 1))
                for par, q in enumerate((qe, qo)):
                    for g in range(KT):
                        o = (2 * par + g) * P
                        last = nc.tensor.matmul(ps_s[r % 2][:, o:o + P],
                                                qk[rows, t % 2, (KT + g) * P:(KT + g + 1) * P],
                                                q[rows, t % 2, g * P:(g + 1) * P], start=True, stop=True)
                last.then_inc(sc_ps, 1)

            def transpose_keys(t):
                for g in range(KT):
                    last = nc.tensor.transpose(ps_tr[:, g * P:(g + 1) * P],
                                               qk[:, t % 2, (KT + g) * P:(KT + g + 1) * P], ident)
                last.then_inc(kt_ps, 1)

            def from_state(t):
                if t >= 1:
                    pe.wait_ge(yn_sb, t)
                else:
                    pe.wait_ge(mask_sb, 1)
                if t == T_RANK:
                    route_ranks()
                    pe.wait_ge(rank_sb, 1)
                if t == T_INVERT:
                    route_inverse()
                    pe.wait_ge(inv_sb, 1)
                if t == T_EXPERT:
                    pe.wait_ge(eid_in, 1)
                    nc.tensor.matmul(ps_y[0:1, D:D + NB], eid[:, :], ident[:, 0:NB], start=True, stop=True).then_inc(eid_ps, 1)
                    pe.wait_ge(eid_sb, 1)
                if t % CPB == 0:
                    return
                pe.wait_ge(st_sb, states_before(t))
                for g in range(KT):
                    nc.tensor.matmul(ps_y[:, g * P:(g + 1) * P], qd[:, t % 2, g * P:(g + 1) * P],
                                     state[:, g * P:(g + 1) * P], start=(g == 0), stop=False, skip_group_check=True)

            def chunk_products(t):
                pe.wait_ge(kt_sb, states_before(t) + 1)
                pe.wait_ge(vg_sb, 2 * (t + 1))
                if t >= 2:
                    pe.wait_ge(res_sb, t - 1)
                for g in range(KT):
                    last = nc.tensor.matmul(ps_po[:, g * P:(g + 1) * P], ktok[:, g * P:(g + 1) * P],
                                            v[:, t % 2, g * P:(g + 1) * P], start=True, stop=True)
                last.then_inc(pr_ps, 1)

            def weigh_values(t, r):
                pe.wait_ge(sc_sb, 4 * t + r + 1)
                if r == 0:
                    pe.wait_ge(vg_sb, 2 * (t + 1))
                for s in range(4 * r, 4 * r + 4):
                    f = HD * head_of_slot(s)
                    last = nc.tensor.matmul(ps_y[:, f:f + HD], st[:, s * P:(s + 1) * P], v[:, t % 2, f:f + HD],
                                            start=(s == 0 and t % CPB == 0), stop=(s == H - 1), skip_group_check=True)
                if r == 3:
                    last.then_inc(y_ps, 1)

            def transpose_back(t):
                pe.wait_ge(hs_sb, t + 1)
                pe.wait_ge(z_sb, t + 1)
                nc.tensor.transpose(ps_tr[:, 0:P], hs[:, t % 2, 0:P], ident)
                nc.tensor.transpose(ps_tr[0:I2, P:2 * P], hs[:, t % 2, P:I], ident)
                for g in range(KT):
                    last = nc.tensor.transpose(ps_tr[:, (2 + g) * P:(3 + g) * P], z[:, t % 2, g * P:(g + 1) * P], ident)
                last.then_inc(trb_ps, 1)

            def project_out(t):
                pe.wait_ge(trb_sb, 3 * (t + 1))
                pe.wait_ge(st_sb, states_before(min(t + 2, NT)))
                if t >= 1:
                    pe.wait_ge(res_sb, t)
                o = ps_po[:, D:2 * D]
                for g in range(KT):
                    nc.tensor.matmul(o, zT[:, g * P:(g + 1) * P], wo[:, g, :], start=(g == 0), stop=False)
                nc.tensor.matmul(o, hT1[:, :], wsd1[:, :], start=False, stop=False)
                nc.tensor.matmul(o, hT2[:, :], wsd2[:, :], start=False, stop=True).then_inc(o_ps, 1)

            pe.wait_ge(wq_in, 16)
            project_qk(0)
            project_vg(0)
            project_shared(0)
            for t in range(NT):
                more = t + 1 < NT
                scores(t, 0)
                scores(t, 1)
                if t % CPB < CPB - 1:
                    transpose_keys(t)
                if more:
                    project_qk(t + 1)
                scores(t, 2)
                from_state(t)
                if t % CPB < CPB - 1:
                    chunk_products(t)
                scores(t, 3)
                if more:
                    project_vg(t + 1)
                weigh_values(t, 0)
                weigh_values(t, 1)
                if t >= 1:
                    if t % CPB < CPB - 1:
                        pe.wait_ge(kt_sb, states_before(t) + 1)
                    transpose_back(t - 1)
                if more:
                    project_shared(t + 1)
                weigh_values(t, 2)
                weigh_values(t, 3)
                if t >= 1:
                    project_out(t - 1)
            transpose_back(NT - 1)
            project_out(NT - 1)
            pe.wait_ge(res_sb, NT)

            def step(q, u, i):
                n = RING * q + u
                if live(i, 0):
                    need(pe, tok_in[u], 16 * (q + 1))
                    need(pe, xt_sb, n - 1)
                    for g in range(KT):
                        last = nc.tensor.transpose(ps_xt[u % 2][:, g * P:(g + 1) * P], xg[:, u, g * P:(g + 1) * P], ident)
                    last.then_inc(xt_ps, 1)
                if live(i, 1):
                    if i == 1:
                        pe.wait_ge(we_in, 16 * (LATE // 5 + 1))
                    e = expert(n - 1)
                    need(pe, xt_sb, n)
                    need(pe, eh_sb, n - 2)
                    for g in range(KT):
                        last = nc.tensor.matmul(ps_gu[(u - 1) % 2][:, 0:2 * I], xbT[:, (u - 1) % 2, g * P:(g + 1) * P],
                                                w1[:, bass.ds(e * EW + g * 2 * I, 2 * I)],
                                                start=(g == 0), stop=(g == KT - 1))
                    last.then_inc(gu_ps, 1)
                if live(i, 2):
                    need(pe, eh_sb, n - 1)
                    need(pe, eht_sb, n - 3)
                    for g in range(KT):
                        last = nc.tensor.transpose(ps_eht[u % 2][:, g * P:(g + 1) * P], eh[:, u % 2, g * P:(g + 1) * P], ident)
                    last.then_inc(eht_ps, 1)
                if live(i, 3):
                    e = expert(n - 3)
                    need(pe, eht_sb, n - 2)
                    need(pe, ys_sb, n - 4)
                    nc.tensor.matmul(ps_dn[(u - 3) % 2][:, 0:D], ehT[:, (u - 3) % 2, 0:P],
                                     w1[:, bass.ds(e * EW + KT * 2 * I, D)], start=True, stop=False)
                    nc.tensor.matmul(ps_dn[(u - 3) % 2][:, 0:D], ehT[0:I2, (u - 3) % 2, P:2 * P],
                                     w2[0:I2, bass.ds(e * D, D)], start=False, stop=True).then_inc(dn_ps, 1)

            def expert(b):
                return pe.value_load(eid_row[0:1, bass.ds(b, 1)], min_val=0, max_val=E - 1)

            expert_loop(pe, step, lambda: pe.wait_ge(wl_in, 16 * ((E - LATE + 3) // 4 + 1)))


def expert_weights(a):
    gu = np.concatenate([a["ffn_gate_w"], a["ffn_up_w"]], axis=1).transpose(2, 0, 1)
    gu = gu.reshape(KT, P, E, 2 * I).transpose(1, 2, 0, 3).reshape(P, E, KT * 2 * I)
    down = a["ffn_down_w"][:, :, :P].transpose(2, 0, 1)
    return np.ascontiguousarray(np.concatenate([gu, down], axis=2)).reshape(P, E * EW)


def kernel(**inp):
    import concourse.bacc as bacc
    from concourse.bass_utils import run_bass_kernel_spmd

    a = {k[3:]: np.asarray(v) for k, v in inp.items()}

    def by_rows(w):
        return np.ascontiguousarray(w.reshape(-1, P, w.shape[1]).transpose(1, 0, 2))

    consts, decay = constants()
    arrays = {
        "x": a["attn_x"],
        "consts": consts,
        "decay": decay,
        "w_router": by_rows(a["ffn_router_w"].T),
        "w_qkvg": by_rows(np.concatenate([a["attn_w" + n].T for n in "qkvg"], axis=1)),
        "w_out": by_rows(a["attn_wo"].T),
        "w_sgu": by_rows(np.concatenate([a["ffn_shared_gate_w"].T, a["ffn_shared_up_w"].T], axis=1)),
        "w_sd1": np.ascontiguousarray(a["ffn_shared_down_w"].T[:P]),
        "w_sd2": np.ascontiguousarray(a["ffn_shared_down_w"].T[P:]),
        "lnwb": np.stack([a["attn_ln_w"], a["attn_ln_b"]]),
        "rbias": a["ffn_router_b"],
        "w_exp": expert_weights(a),
        "w_exp2": np.ascontiguousarray(a["ffn_down_w"][:, :, P:].transpose(2, 0, 1)).reshape(I2, E * D),
    }
    nc = bacc.Bacc("TRN2", target_bir_lowering=False, num_devices=1)
    args = [nc.dram_tensor(n + "_dram", v.shape, F32, kind="ExternalInput").ap() for n, v in arrays.items()]
    out = nc.dram_tensor("out_dram", (BATCH, SEQ, D), F32, kind="ExternalOutput").ap()
    xn_rows = nc.dram_tensor("xn_rows", (TOK, D), F32, kind="Internal").ap()
    y_rows = nc.dram_tensor("y_rows", (ROWS, D), F32, kind="Internal").ap()
    build(nc, *args, xn_rows, y_rows, out)
    r = run_bass_kernel_spmd(nc, [{n + "_dram": v for n, v in arrays.items()}], core_ids=[0])
    return r.results[0]["out_dram"]
```

```python
from contextlib import ExitStack

import numpy as np

import concourse.bass as bass
from concourse import mybir

F32 = mybir.dt.float32
BF16 = mybir.dt.bfloat16
U32 = mybir.dt.uint32
I32 = mybir.dt.int32
ALU = mybir.AluOpType
ACT = mybir.ActivationFunctionType
AX_X = mybir.AxisListType.X

P = 128
BATCH, SEQ, D = 2, 512, 256
TOK = BATCH * SEQ
NT = TOK // P
CPB = SEQ // P
KT = D // P
H, HD = 16, 16
HG = P // HD
SCALE = HD ** -0.5
EPS = 1e-5
E, TOPK, I = 32, 4, 192
I2 = I - P
RSCALE = 1.8
RSQRT_MAGIC = 0x5F3759DF
EW = KT * 2 * I + D
ROWS = TOK * TOPK
RING = 4
NB = -(-(E + (ROWS - 1) // P) // RING) * RING
FEWEST = E // RING
MAXB = TOK // P
NA = NT * TOPK
LATE = 15
Q_FIRST = 2
Q_LATE = (LATE + 1) // RING
Q_END = NB // RING
T_RANK, T_INVERT, T_EXPERT = 1, 4, 5
LAG = 7

C_ID = 0
C_BM = C_ID + P
C_QD = C_BM + P
C_KD = C_QD + KT * P
C_GC = C_KD + H
C_PM = C_GC + KT
C_IO = C_PM + 2
C_PI = C_IO + P
C_FILL = C_PI + 1
C_TK = C_FILL + 1
C_LT = C_TK + NA
C_END = C_LT + P


def head_of_slot(s):
    r, par, g = s // 4, s // 2 % 2, s % 2
    return HG * g + 2 * r + par


def constants():
    gammas = (1.0 - np.exp(np.linspace(np.log(1 / 32), np.log(1 / 64), H)).astype(np.float32)).astype(np.float64)
    i = np.arange(P)
    c = np.zeros((P, C_END))
    c[:, C_ID:C_ID + P] = np.eye(P)
    c[:, C_BM:C_BM + P] = i[:, None] // HD == i[None, :] // HD
    for g in range(KT):
        row_gamma = gammas[HG * g + i // HD]
        c[:, C_QD + g * P:C_QD + (g + 1) * P] = SCALE * row_gamma[:, None] ** (i[None, :] + 1)
        c[:, C_GC + g] = row_gamma ** P
    c[:, C_KD:C_KD + H] = gammas[None, :] ** (P - 1 - i[:, None])
    for par in range(2):
        c[:, C_PM + par] = i // HD % 2 == par
    c[:, C_IO:C_IO + P] = i[None, :]
    c[:, C_PI] = i
    c[:, C_FILL] = ROWS + P + i
    for t in range(NT):
        for k in range(TOPK):
            c[:, C_TK + t * TOPK + k] = 1 + k * NT + t
    c[:, C_LT:C_LT + P] = i[:, None] < i[None, :]
    dist = i[None, :] - i[:, None]
    decay = np.zeros((P, H, P))
    for s in range(H):
        decay[:, s] = np.where(dist >= 0, SCALE * gammas[head_of_slot(s)] ** np.maximum(dist, 0), 0.0)
    return c.astype(np.float32), decay.reshape(P, H * P).astype(np.float32)


def build(nc, x, consts, decay, w_router, w_qkvg, w_out, w_sgu, w_sd1, w_sd2, lnwb, rbias, w_exp, w_exp2, xn_rows, y_rows, out):
    with ExitStack() as ctx:
        def sb(name, shape, dt=F32):
            return ctx.enter_context(nc.sbuf_tensor(name, shape, dt))

        def sem(name):
            return ctx.enter_context(nc.semaphore(name))

        w1 = sb("w1", [P, E * EW])
        w2 = sb("w2", [P, E * D])
        free1, free2 = [LATE * EW], [LATE * D]

        def early(*shape, dt=F32, of=w1, free=free1):
            n = int(np.prod(shape)) * mybir.dt.size(dt) // 4
            ap = of[:, free[0]:free[0] + n]
            free[0] += n
            assert free[0] <= of.shape[1]
            if dt != F32:
                ap = ap.bitcast(dt)
            if len(shape) == 2:
                ap = ap.rearrange("p (a b) -> p a b", a=shape[0])
            return ap

        x_sb = sb("x_sb", [P, NT, D])
        cst = sb("cst", [P, C_END])
        rw = sb("rw", [P, NA])
        codes = sb("codes", [P, NB + RING, 2], U32)
        eid_row = sb("eid_row", [1, NB + 1], I32)

        VG = HG * (P + HD)
        vz = early(KT * VG)
        xn = vz[:, 0:NT * D].rearrange("p (t d) -> p t d", t=NT)
        xnT = early(KT, TOK)
        dec = early(H * P)
        wqkvg = early(KT, 4 * D)
        st = early(H * P)
        wo = early(KT, D)
        wsgu = early(KT, 2 * I)
        wsd1 = early(D)
        lnw = early(D)
        lnb = early(D)
        wr = early(KT, E)
        rb = early(E)
        qk = early(2, 4 * P)
        qe = early(2, KT * P)
        qo = early(2, KT * P)
        qd = early(2, KT * P)
        v = early(2, D)
        wsd2 = sb("wsd2", [I2, D])
        stats = sb("stats", [P, NT, 6])
        mv = sb("mv", [P, NT, 2])
        rstd = sb("rstd", [P, NT])
        var = sb("var", [P, NT])
        newton = sb("newton", [P, NT])
        gate = early(3, D)
        ktok = sb("ktok", [P, D])
        state_mem = sb("state_mem", [P, 2 * KT * P])
        state = state_mem[:, 0:KT * P]
        pmask = state_mem[:, KT * P:2 * KT * P]
        ystats = sb("ystats", [P, 6])
        ymv = sb("ymv", [P, 2])
        yrstd = sb("yrstd", [P, 1])
        yn = sb("yn", [P, 2, D])
        z1 = sb("z1", [P, D])
        z = early(2, D)
        sgs = sb("sgs", [P, I])
        hs = sb("hs", [P, 2, I])
        yT = sb("yT", [P, KT * P])
        zT = sb("zT", [P, KT * P])
        hT1 = sb("hT1", [P, P])
        hT2 = sb("hT2", [I2, P])

        logits = sb("logits", [P, NT, E])
        top = sb("top", [P, NT, 8])
        topi = sb("topi", [P, NT, 8], U32)
        topf = sb("topf", [P, NT, TOPK])
        ex = sb("ex", [P, NT, TOPK])
        exs = sb("exs", [P, NT])
        chosen = sb("chosen", [P, NA, E], BF16)
        mask = sb("mask", [P, NT, E], BF16)
        lt_bf = sb("lt_bf", [P, P], BF16)
        ones_bf = sb("ones_bf", [P, P], BF16)
        ranks = sb("ranks", [P, NT, E])
        counts = sb("counts", [P, E])
        over = sb("over", [P, E, MAXB - 1], BF16)
        nblk = sb("nblk", [P, E])
        ends = sb("ends", [P, E])
        ones_e = sb("ones_e", [P, E])
        base = sb("base", [P, E])
        slot_k = sb("slot_k", [P, NA])
        slot_i = sb("slot_i", [P, NA], U32)
        blk_i = sb("blk_i", [P, NA], U32)
        pos_i = sb("pos_i", [P, NA], U32)
        blk_f = sb("blk_f", [P, NA])
        pos_f = sb("pos_f", [P, NA])
        prod = early(NA, E, of=w2, free=free2)
        pos_hot = early(NA, P, dt=BF16, of=w2, free=free2)
        blk_hot = early(NA, NB, dt=BF16, of=w2, free=free2)
        loop_mem = sb("loop_mem", [P, RING * D + 2 * KT * P + 2 * I + 2 * NB])
        blk_code = loop_mem[:, 0:NA * NB].bitcast(BF16).rearrange("p (a b) -> p a b", a=NA)

        xg = sb("xg", [P, RING, D])
        xbT = sb("xbT", [P, 2, KT * P])
        eh = state_mem[:, 0:2 * I].rearrange("p (a b) -> p a b", a=2)
        gidx = sb("gidx", [P, RING], U32)
        sidx = sb("sidx", [P, RING], U32)
        ysb = loop_mem[:, 0:RING * D].rearrange("p (a b) -> p a b", a=RING)
        ehT = loop_mem[:, RING * D:RING * D + 2 * KT * P].rearrange("p (a b) -> p a b", a=2)
        sil = loop_mem[:, RING * D + 2 * KT * P:RING * D + 2 * KT * P + 2 * I].rearrange("p (a b) -> p a b", a=2)
        back = w1[:, 0:NA * D].rearrange("p (t k d) -> p t k d", t=NT, k=TOPK)
        inv = sb("inv", [P, 2 * NB])
        unused = sb("unused", [P, NB])
        code_f = sb("code_f", [P, NB])
        le = sb("le", [P, E])
        rounds_i = sb("rounds_i", [1, 1], I32)
        eid = sb("eid", [P, 1])

        bank = [ctx.enter_context(nc.psum_tensor(f"bank{i}", [P, 512], F32)) for i in range(8)]
        ps_tr, ps_qk, ps_vg, ps_sg, ps_s0, ps_s1, ps_y, ps_po = bank
        ps_s = [ps_s0, ps_s1]
        ps_xt, ps_gu, ps_eht, ps_dn = [ps_qk, ps_vg], [ps_sg, ps_s0], [ps_s1, ps_tr], [ps_y, ps_po]

        ident = cst[:, C_ID:C_ID + P]

        x_in = [sem(f"x_in{i}") for i in range(2)]
        c_in = sem("c_in")
        w_in = sem("w_in")
        wq_in = sem("wq_in")
        d_in = sem("d_in")
        dve_step = sem("dve_step")
        pool_seq = sem("pool_seq")
        xn_done = sem("xn_done")
        xnT_ps = sem("xnT_ps")
        xnT_sb = sem("xnT_sb")
        lg_ps = sem("lg_ps")
        lg_sb = sem("lg_sb")
        qk_ps = sem("qk_ps")
        qk_sb = sem("qk_sb")
        q_ready = sem("q_ready")
        vz_sb = sem("vz_sb")
        yt_sb = sem("yt_sb")
        yt_ps = sem("yt_ps")
        vg_ps = sem("vg_ps")
        vg_sb = sem("vg_sb")
        sg_ps = sem("sg_ps")
        sgs_sb = sem("sgs_sb")
        hs_sb = sem("hs_sb")
        sc_ps = sem("sc_ps")
        sc_sb = sem("sc_sb")
        kt_ps = sem("kt_ps")
        kt_sb = sem("kt_sb")
        pr_ps = sem("pr_ps")
        st_sb = sem("st_sb")
        y_ps = sem("y_ps")
        yn_sb = sem("yn_sb")
        z_sb = sem("z_sb")
        trb_ps = sem("trb_ps")
        trb_sb = sem("trb_sb")
        o_ps = sem("o_ps")
        res_sb = sem("res_sb")
        out_done = sem("out_done")
        xn_out = sem("xn_out")
        we_in = sem("we_in")
        wl_in = [sem(f"wl_in{i}") for i in range(2)]
        pool_cst = sem("pool_cst")
        soft_in = sem("soft_in")
        soft_ex = sem("soft_ex")
        mask_sb = sem("mask_sb")
        rank_ps = sem("rank_ps")
        rank_sb = sem("rank_sb")
        hot_sb = sem("hot_sb")
        inv_ps = sem("inv_ps")
        inv_sb = sem("inv_sb")
        eid_ps = sem("eid_ps")
        eid_in = sem("eid_in")
        eid_sb = sem("eid_sb")
        gidx_sb = sem("gidx_sb")
        pool_go = sem("pool_go")
        tok_in = [sem(f"tok_in{i}") for i in range(RING)]
        xt_ps = sem("xt_ps")
        xt_sb = sem("xt_sb")
        gu_ps = sem("gu_ps")
        sil_sb = sem("sil_sb")
        eh_sb = sem("eh_sb")
        eht_ps = sem("eht_ps")
        eht_sb = sem("eht_sb")
        dn_ps = sem("dn_ps")
        ys_sb = sem("ys_sb")
        sent = [sem(f"sent{i}") for i in range(RING)]
        back_in = [sem(f"back_in{i}") for i in range(NT)]
        tot_sb = sem("tot_sb")

        block = ctx.enter_context(nc.Block())
        x_v = x.rearrange("b (t p) d -> p (b t) d", p=P)
        out_v = out.rearrange("b (t p) d -> p (b t) d", p=P)

        def states_before(t):
            return sum(1 for u in range(t) if u % CPB < CPB - 1)

        def need(eng, semaphore, value):
            if not isinstance(value, int) or value > 0:
                eng.wait_ge(semaphore, value)

        def filled_rounds(eng):
            eng.wait_ge(eid_sb, 1)
            return FEWEST + eng.value_load(eid_row[0:1, NB:NB + 1], min_val=0, max_val=Q_END - FEWEST)

        def expert_loop(eng, step, between={}, before_late=None):
            for i in range(RING * Q_FIRST):
                step(i // RING, i % RING, i)
                if i in between:
                    between[i]()
            with eng.Fori(Q_FIRST, Q_LATE) as q:
                for u in range(RING):
                    step(q, u, None)
            if before_late:
                before_late()
            rounds = filled_rounds(eng)
            with eng.Fori(Q_LATE, Q_END) as q:
                with eng.If(q < rounds):
                    for u in range(RING):
                        step(q, u, None)
            for u in range(3):
                step(rounds, u, NB + u)

        def live(i, stage):
            return i is None or 0 <= i - stage < NB

        @block.sync
        def _(sp):
            for half in range(2):
                s = slice(half * NT // 2, (half + 1) * NT // 2)
                sp.dma_start(x_sb[:, s, :], x_v[:, s, :]).then_inc(x_in[half], 16)
            sp.dma_start(wqkvg[:, :, :], w_qkvg).then_inc(wq_in, 16)
            sp.dma_start(wsgu[:, :, :], w_sgu).then_inc(wq_in, 16)
            sp.dma_start(dec[:, :], decay).then_inc(d_in, 16)
            for half in range(2):
                s = slice(half * NT // 2, (half + 1) * NT // 2)
                sp.wait_ge(xn_done, (half + 1) * NT // 2)
                sp.dma_start(xn_rows.rearrange("(t p) d -> p t d", p=P)[:, s, :], xn[:, s, :]).then_inc(xn_out, 16)
            for e in range(0, LATE, 5):
                sp.dma_start(w1[:, e * EW:(e + 5) * EW], w_exp[:, e * EW:(e + 5) * EW]).then_inc(we_in, 16)
            sp.dma_start(w2[0:I2, 0:LATE * D], w_exp2[:, 0:LATE * D]).then_inc(we_in, 16)
            sp.wait_ge(xn_out, 32)
            sp.wait_ge(res_sb, NT)
            sp.dma_start(w2[0:I2, LATE * D:E * D], w_exp2[:, LATE * D:E * D]).then_inc(wl_in[0], 16)
            for n, e in enumerate(range(LATE, E), 1):
                if n >= 2:
                    sp.wait_ge(wl_in[n % 2], 16 * (n // 2))
                sp.dma_start(w1[:, e * EW:(e + 1) * EW], w_exp[:, e * EW:(e + 1) * EW]).then_inc(wl_in[n % 2], 16)
            rounds = filled_rounds(sp)
            for s in range(RING):
                sp.wait_ge(sent[s], 16 * rounds)
            y_v = y_rows.rearrange("(k t p) d -> t p k d", t=NT, p=P)
            for t in range(NT):
                sp.dma_start(back[:, t], y_v[t]).then_inc(back_in[t], 16)
            for t in range(NT):
                sp.wait_ge(tot_sb, t + 1)
                sp.dma_start(out_v[:, t, :], x_sb[:, t, :]).then_inc(out_done, 16)
            sp.wait_ge(out_done, 16 * NT)

        @block.scalar
        def _(act):
            act.dma_start(cst[:, :], consts).then_inc(c_in, 16)
            act.dma_start(wr[:, :, :], w_router).then_inc(c_in, 16)
            act.dma_start(rb[:, :], rbias.partition_broadcast(P)).then_inc(c_in, 16)
            act.dma_start(wo[:, :, :], w_out).then_inc(w_in, 16)
            act.dma_start(wsd1[:, :], w_sd1).then_inc(w_in, 16)
            act.dma_start(wsd2[:, :], w_sd2).then_inc(w_in, 16)
            act.dma_start(lnw[:, :], lnwb[0].partition_broadcast(P)).then_inc(w_in, 16)
            act.dma_start(lnb[:, :], lnwb[1].partition_broadcast(P)).then_inc(w_in, 16)

            for u in range(NT // 2):
                act.wait_ge(xnT_ps, u + 1)
                nc.scalar.copy(xnT[:, :, 2 * u * P:2 * (u + 1) * P],
                               ps_s[u % 2][:, :].rearrange("p (g n) -> p g n", g=KT)).then_inc(xnT_sb, 1)

            def take_projections(t):
                act.wait_ge(qk_ps, t + 1)
                nc.scalar.copy(qk[:, t % 2, :], ps_qk[:, :]).then_inc(qk_sb, 1)
                act.wait_ge(vg_ps, t + 1)
                nc.scalar.copy(v[:, t % 2, :], ps_vg[:, 0:D]).then_inc(vg_sb, 1)
                nc.scalar.activation(gate[:, t % 3, :], ps_vg[:, D:2 * D], ACT.Silu).then_inc(vg_sb, 1)

            def take_shared_gate(t):
                act.wait_ge(sg_ps, t + 1)
                nc.scalar.activation(sgs[:, :], ps_sg[:, 0:I], ACT.Silu).then_inc(sgs_sb, 1)

            def take_transposed(t):
                act.wait_ge(trb_ps, t + 1)
                nc.scalar.copy(hT1[:, :], ps_tr[:, 0:P]).then_inc(trb_sb, 1)
                nc.scalar.copy(hT2[:, :], ps_tr[0:I2, P:2 * P]).then_inc(trb_sb, 1)
                nc.scalar.copy(zT[:, :], ps_tr[:, 2 * P:4 * P]).then_inc(trb_sb, 1)

            def take_outputs(t):
                act.wait_ge(y_ps, t + 1)
                nc.scalar.copy(yT[:, :], ps_y[:, 0:D]).then_inc(yt_sb, 1)

            act.wait_ge(soft_in, 1)
            nc.scalar.activation(ex[:, :, :], ex[:, :, :], ACT.Exp).then_inc(soft_ex, 1)
            take_projections(0)
            take_shared_gate(0)
            for t in range(NT):
                if t + 1 < NT:
                    take_projections(t + 1)
                if t >= 1:
                    take_transposed(t - 1)
                if t + 1 < NT:
                    take_shared_gate(t + 1)
                take_outputs(t)

            def step(q, u, i):
                n = RING * q + u
                if live(i, 0):
                    need(act, xt_ps, n + 1)
                    need(act, gu_ps, n - 1)
                    nc.scalar.copy(xbT[:, u % 2, :], ps_xt[u % 2][:, 0:KT * P]).then_inc(xt_sb, 1)
                if live(i, 1):
                    need(act, gu_ps, n)
                    need(act, eh_sb, n - 2)
                    nc.scalar.activation(sil[:, (u - 1) % 2, :], ps_gu[(u - 1) % 2][:, 0:I], ACT.Silu).then_inc(sil_sb, 1)
                if live(i, 2):
                    need(act, eht_ps, n - 1)
                    need(act, dn_ps, n - 3)
                    nc.scalar.copy(ehT[:, u % 2, :], ps_eht[u % 2][:, 0:KT * P]).then_inc(eht_sb, 1)

            expert_loop(act, step, {2: lambda: take_transposed(NT - 1)})

        @block.gpsimd
        def _(pool):
            steps = [0]

            def step(ins):
                steps[0] += 1
                ins.then_inc(pool_seq, 1)
                pool.wait_ge(pool_seq, steps[0])

            def mask_queries(t):
                pool.wait_ge(qk_sb, t + 1)
                if t == 0:
                    pool.wait_ge(c_in, 48)
                q = qk[:, t % 2, 0:KT * P]
                nc.gpsimd.tensor_scalar(qe[:, t % 2, :], q, cst[:, C_PM:C_PM + 1], None, ALU.mult).then_inc(q_ready, 1)
                nc.gpsimd.tensor_scalar(qo[:, t % 2, :], q, cst[:, C_PM + 1:C_PM + 2], None, ALU.mult).then_inc(q_ready, 1)
                nc.gpsimd.tensor_tensor(qd[:, t % 2, :], q, cst[:, C_QD:C_QD + KT * P], ALU.mult).then_inc(q_ready, 1)

            def gate_output(t):
                pool.wait_ge(yn_sb, t + 1)
                if t == 0:
                    pool.wait_ge(w_in, 80)
                step(nc.gpsimd.tensor_tensor(z1[:, :], yn[:, t % 2, :], lnw[:, :], ALU.mult))
                step(nc.gpsimd.tensor_tensor(z1[:, :], z1[:, :], lnb[:, :], ALU.add))
                pool.wait_ge(vg_sb, 2 * (t + 1))
                nc.gpsimd.tensor_tensor(z[:, t % 2, :], z1[:, :], gate[:, t % 3, :], ALU.mult).then_inc(z_sb, 1)

            def pool_step(q, u, j):
                n = RING * q + u
                if live(j, 0):
                    need(pool, gidx_sb, n + 1)
                    pool.sem_inc(pool_go, 1)
                    need(pool, xt_ps, n - RING + 1)
                    pool.sem_inc(pool_go, 1)
                    nc.gpsimd.indirect_dma_start(
                        xg[:, u, :], None, xn_rows, bass.IndirectOffsetOnAxis(ap=gidx[:, u:u + 1], axis=0),
                    ).then_inc(tok_in[u], 16)
                if live(j, LAG):
                    w = (u - LAG) % RING
                    need(pool, ys_sb, n - LAG + 1)
                    pool.sem_inc(pool_go, 1)
                    nc.gpsimd.indirect_dma_start(
                        y_rows, bass.IndirectOffsetOnAxis(ap=sidx[:, w:w + 1], axis=0), ysb[:, w, :], None,
                        bounds_check=ROWS - 1, oob_is_err=False,
                    ).then_inc(sent[w], 16)

            def spread_values(t):
                pool.wait_ge(vg_sb, 2 * (t + 1))
                if t >= 1:
                    pool.wait_ge(y_ps, t)
                nc.gpsimd.tensor_copy(vz[:, :].rearrange("p (h c) -> p h c", c=P + HD)[:, :, 0:HD],
                                      v[:, t % 2, :].rearrange("p (h d) -> p h d", d=HD)).then_inc(vz_sb, 1)

            pool.wait_ge(c_in, 48)
            nc.gpsimd.memset(ones_bf[:, :], 1.0)
            nc.gpsimd.memset(ones_e[:, :], 1.0)
            nc.gpsimd.tensor_copy(lt_bf[:, :], cst[:, C_LT:C_LT + P]).then_inc(pool_cst, 1)
            pool.wait_ge(xn_out, 32)
            pool.wait_ge(xnT_ps, NT // 2)
            step(nc.gpsimd.memset(vz[:, :], 0.0))
            mask_queries(0)
            for t in range(NT):
                spread_values(t)
                if t + 1 < NT:
                    mask_queries(t + 1)
                if t >= 1:
                    gate_output(t - 1)
            for j in range(RING):
                pool_step(0, j, j)
            gate_output(NT - 1)
            for j in range(RING, Q_FIRST * RING):
                pool_step(j // RING, j % RING, j)
            rounds = filled_rounds(pool)
            with pool.Fori(Q_FIRST, Q_END) as q:
                with pool.If(q < rounds):
                    for u in range(RING):
                        pool_step(q, u, None)
            for j in range(LAG):
                pool_step(rounds + j // RING, j % RING, NB + j)

        @block.vector
        def _(dve):
            steps = [0]

            def step(ins):
                steps[0] += 1
                ins.then_inc(dve_step, 1)
                dve.wait_ge(dve_step, steps[0])

            def inverse_sqrt(y, variance, v, a, between=()):
                fill = iter(between)

                def link(ins):
                    steps[0] += 1
                    ins.then_inc(dve_step, 1)
                    next(fill, lambda: None)()
                    dve.wait_ge(dve_step, steps[0])

                link(nc.vector.tensor_scalar(v, variance, EPS, None, ALU.add))
                link(nc.vector.tensor_scalar(a.bitcast(I32), v.bitcast(I32), 1, None, ALU.logical_shift_right))
                link(nc.vector.tensor_scalar(y.bitcast(I32), a.bitcast(I32), -1, RSQRT_MAGIC, ALU.mult, ALU.add))
                for _ in range(3):
                    if y.shape[-1] == 1:
                        link(nc.vector.scalar_tensor_tensor(a, y, y, v, ALU.mult, ALU.mult))
                    else:
                        link(nc.vector.tensor_tensor(a, y, y, ALU.mult))
                        link(nc.vector.tensor_tensor(a, a, v, ALU.mult))
                    link(nc.vector.tensor_scalar(a, a, -0.5, 1.5, ALU.mult, ALU.add))
                    link(nc.vector.tensor_tensor(y, y, a, ALU.mult))
                for f in fill:
                    f()

            def moments(t):
                nc.vector.bn_stats(stats[:, t, :], x_sb[:, t, :])

            def normalise(t):
                nc.vector.tensor_scalar(xn[:, t, :], x_sb[:, t, :], mv[:, t, 0:1], rstd[:, t:t + 1],
                                        ALU.subtract, ALU.mult).then_inc(xn_done, 1)

            h = NT // 2
            dve.wait_ge(x_in[0], 16)
            for t in range(h):
                last = nc.vector.bn_stats(stats[:, t, :], x_sb[:, t, :])
            step(last)
            for t in range(h):
                last = nc.vector.bn_aggr(mv[:, t, :], stats[:, t, :])
            step(last)
            dve.wait_ge(x_in[1], 16)
            inverse_sqrt(rstd[:, 0:h], mv[:, 0:h, 1], var[:, 0:h], newton[:, 0:h],
                         [lambda t=t: moments(t) for t in range(h, NT)])
            for t in range(h, NT):
                last = nc.vector.bn_aggr(mv[:, t, :], stats[:, t, :])
            step(last)
            inverse_sqrt(rstd[:, h:NT], mv[:, h:NT, 1], var[:, h:NT], newton[:, h:NT],
                         [lambda t=t: normalise(t) for t in range(h)])
            for t in range(h, NT):
                normalise(t)
            dve.wait_ge(lg_ps, NT)
            dve.wait_ge(c_in, 48)
            ins = nc.vector.tensor_tensor(logits[:, :, :], ps_y[:, 0:NT * E].rearrange("p (t e) -> p t e", t=NT),
                                          rb[:, :].unsqueeze(1).broadcast_to([P, NT, E]), ALU.add)
            step(ins)

            for t in range(NT):
                last = nc.vector.max(top[:, t, :], logits[:, t, :])
            step(last)
            for t in range(NT):
                last = nc.vector.max_index(topi[:, t, :], top[:, t, :], logits[:, t, :])
            step(last)
            nc.vector.tensor_tensor(ex[:, :, :], top[:, :, 0:TOPK], top[:, :, 0:1].broadcast_to([P, NT, TOPK]),
                                    ALU.subtract).then_inc(soft_in, 1)
            step(nc.vector.tensor_copy(topf[:, :, :], topi[:, :, 0:TOPK]))
            step(nc.vector.tensor_tensor(
                chosen[:, :, :], cst[:, C_IO:C_IO + E].unsqueeze(1).broadcast_to([P, NA, E]),
                topf[:, :, :].rearrange("p t k -> p (t k)").unsqueeze(2).broadcast_to([P, NA, E]), ALU.is_equal))
            with nc.allow_low_precision(reason="the sums are 0 or 1"):
                nc.vector.tensor_reduce(mask[:, :, :], chosen[:, :, :].rearrange("p (t k) e -> p t e k", k=TOPK),
                                        AX_X, ALU.add).then_inc(mask_sb, 1)
            dve.wait_ge(soft_ex, 1)
            step(nc.vector.reduce_sum(exs[:, :], ex[:, :, :], AX_X))
            step(nc.vector.reciprocal(exs[:, :], exs[:, :]))
            nc.vector.scalar_tensor_tensor(rw[:, :].rearrange("p (t k) -> p t k", k=TOPK), ex[:, :, :], RSCALE,
                                           exs[:, :].unsqueeze(2).broadcast_to([P, NT, TOPK]), ALU.mult, ALU.mult)

            def take_ranks():
                dve.wait_ge(rank_ps, 1)
                nc.vector.tensor_copy(ranks[:, :, :], ps_y[:, D:2 * D].rearrange("p (t e) -> p t e", t=NT))
                nc.vector.tensor_scalar(counts[:, :], ps_y[:, 0:E], 1.0 / P, None, ALU.mult).then_inc(rank_sb, 1)

            def assign_slots():
                dve.wait_ge(rank_sb, 1)
                step(nc.vector.tensor_tensor(over[:, :, :], counts[:, :].unsqueeze(2).broadcast_to([P, E, MAXB - 1]),
                                             cst[:, C_IO + 1:C_IO + MAXB].unsqueeze(1).broadcast_to([P, E, MAXB - 1]),
                                             ALU.is_gt))
                step(nc.vector.reduce_sum(nblk[:, :], over[:, :, :], AX_X))
                step(nc.vector.tensor_scalar(nblk[:, :], nblk[:, :], 1.0, None, ALU.add))
                dve.wait_ge(pool_cst, 1)
                step(nc.vector.tensor_tensor_scan(ends[:, :], ones_e[:, :], nblk[:, :], 0.0, ALU.mult, ALU.add))
                step(nc.vector.tensor_tensor(base[:, :], ends[:, :], nblk[:, :], ALU.subtract))
                step(nc.vector.tensor_scalar(base[:, :], base[:, :], float(P), None, ALU.mult))
                step(nc.vector.tensor_tensor(ranks[:, :, :], ranks[:, :, :],
                                             base[:, :].unsqueeze(1).broadcast_to([P, NT, E]), ALU.add))
                step(nc.vector.tensor_tensor(
                    prod[:, :, :].rearrange("p (t k) e -> p t k e", k=TOPK),
                    chosen[:, :, :].rearrange("p (t k) e -> p t k e", k=TOPK),
                    ranks[:, :, :].unsqueeze(2).broadcast_to([P, NT, TOPK, E]), ALU.mult))
                step(nc.vector.reduce_sum(slot_k[:, :], prod[:, :, :], AX_X))
                step(nc.vector.tensor_copy(slot_i[:, :], slot_k[:, :]))
                step(nc.vector.tensor_scalar(blk_i[:, :], slot_i[:, :], P.bit_length() - 1, None,
                                             ALU.logical_shift_right))
                step(nc.vector.tensor_scalar(pos_i[:, :], slot_i[:, :], P - 1, None, ALU.bitwise_and))
                nc.vector.tensor_copy(blk_f[:, :], blk_i[:, :])
                step(nc.vector.tensor_copy(pos_f[:, :], pos_i[:, :]))

            def one_hot_positions():
                nc.vector.tensor_tensor(pos_hot[:, :, :], cst[:, C_IO:C_IO + P].unsqueeze(1).broadcast_to([P, NA, P]),
                                        pos_f[:, :].unsqueeze(2).broadcast_to([P, NA, P]), ALU.is_equal)

            def one_hot_blocks():
                step(nc.vector.tensor_tensor(blk_hot[:, :, :], cst[:, C_IO:C_IO + NB].unsqueeze(1).broadcast_to([P, NA, NB]),
                                             blk_f[:, :].unsqueeze(2).broadcast_to([P, NA, NB]), ALU.is_equal))
                nc.vector.tensor_tensor(blk_code[:, :, 0:NB], blk_hot[:, :, :],
                                        cst[:, C_TK:C_TK + NA].unsqueeze(2).broadcast_to([P, NA, NB]), ALU.mult)
                nc.vector.tensor_scalar(blk_code[:, :, NB:2 * NB], blk_hot[:, :, :], cst[:, C_PI:C_PI + 1], None,
                                        ALU.mult).then_inc(hot_sb, 1)

            def take_inverse():
                dve.wait_ge(inv_ps, 1)
                nc.vector.tensor_copy(inv[:, :], ps_y[:, D:D + 2 * NB]).then_inc(inv_sb, 1)

            def make_codes():
                dve.wait_ge(inv_sb, 1)
                nc.vector.tensor_scalar(unused[:, :], inv[:, 0:NB], 0.0, cst[:, C_FILL:C_FILL + 1],
                                        ALU.is_equal, ALU.mult)
                nc.vector.memset(codes[:, NB:NB + RING, :], 0)
                step(nc.vector.tensor_scalar(code_f[:, :], inv[:, 0:NB], float(P), float(-P), ALU.mult, ALU.add))
                step(nc.vector.tensor_tensor(code_f[:, :], code_f[:, :], unused[:, :], ALU.add))
                step(nc.vector.tensor_tensor(codes[:, 0:NB, 1], code_f[:, :], inv[:, NB:2 * NB], ALU.add))
                step(nc.vector.tensor_scalar(codes[:, 0:NB, 0], codes[:, 0:NB, 1], TOK - 1, None, ALU.bitwise_and))
                nc.vector.tensor_copy(gidx[:, :], codes[:, 0:RING, 0]).then_inc(gidx_sb, RING)
                step(nc.vector.tensor_scalar(rounds_i[:, :], ends[0:1, E - 1:E], float(RING - 1 - E), None, ALU.add))
                nc.vector.tensor_scalar(eid_row[:, NB:NB + 1], rounds_i[:, :], RING.bit_length() - 1, None,
                                        ALU.logical_shift_right)
                step(nc.vector.tensor_scalar(le[:, :], ends[:, :], cst[:, C_PI:C_PI + 1], None, ALU.is_le))
                step(nc.vector.reduce_sum(eid[:, :], le[:, :], AX_X))
                nc.vector.tensor_scalar(eid[:, :], eid[:, :], float(E - 1), None, ALU.min).then_inc(eid_in, 1)

            def take_block_experts():
                dve.wait_ge(eid_ps, 1)
                nc.vector.tensor_copy(eid_row[:, 0:NB], ps_y[0:1, D:D + NB]).then_inc(eid_sb, 1)

            def decay_scores(t, r):
                dve.wait_ge(sc_ps, 4 * t + r + 1)
                if t == 0 and r == 0:
                    dve.wait_ge(d_in, 16)
                nc.vector.tensor_tensor(st[:, 4 * r * P:4 * (r + 1) * P], ps_s[r % 2][:, :],
                                        dec[:, 4 * r * P:4 * (r + 1) * P], ALU.mult).then_inc(sc_sb, 1)

            def decay_keys(t):
                dve.wait_ge(kt_ps, states_before(t) + 1)
                nc.vector.tensor_tensor(ktok[:, :].rearrange("p (h d) -> p h d", h=H),
                                        ps_tr[:, 0:D].rearrange("p (h d) -> p h d", h=H),
                                        cst[:, C_KD:C_KD + H].unsqueeze(2).broadcast_to([P, H, HD]),
                                        ALU.mult).then_inc(kt_sb, 1)

            def update_state(t):
                dve.wait_ge(pr_ps, states_before(t) + 1)
                first = t % CPB == 0
                to = state if first else pmask
                ins = nc.vector.tensor_tensor(to[:, :].rearrange("p (g n) -> p g n", g=KT),
                                              ps_po[:, 0:KT * P].rearrange("p (g n) -> p g n", g=KT),
                                              cst[:, C_BM:C_BM + P].unsqueeze(1).broadcast_to([P, KT, P]), ALU.mult)
                if first:
                    ins.then_inc(st_sb, 1)
                    return
                step(ins)
                for g in range(KT):
                    s = slice(g * P, (g + 1) * P)
                    last = nc.vector.scalar_tensor_tensor(state[:, s], state[:, s], cst[:, C_GC + g:C_GC + g + 1],
                                                          pmask[:, s], ALU.mult, ALU.add)
                last.then_inc(st_sb, 1)

            def shared_hidden(t):
                dve.wait_ge(sgs_sb, t + 1)
                nc.vector.tensor_tensor(hs[:, t % 2, :], sgs[:, :], ps_sg[:, I:2 * I], ALU.mult).then_inc(hs_sb, 1)

            def add_residual(t):
                dve.wait_ge(o_ps, t + 1)
                nc.vector.tensor_tensor(x_sb[:, t, :], x_sb[:, t, :], ps_po[:, D:2 * D], ALU.add).then_inc(res_sb, 1)

            def normalise_output(t):
                dve.wait_ge(yt_ps, t + 1)
                step(nc.vector.bn_stats(ystats[:, :], ps_y[:, D:2 * D]))
                step(nc.vector.bn_aggr(ymv[:, :], ystats[:, :]))
                inverse_sqrt(yrstd[:, :], ymv[:, 1:2], var[:, 0:1], newton[:, 0:1])
                if t >= 2:
                    dve.wait_ge(z_sb, t - 1)
                nc.vector.tensor_scalar(yn[:, t % 2, :], ps_y[:, D:2 * D], ymv[:, 0:1], yrstd[:, :],
                                        ALU.subtract, ALU.mult).then_inc(yn_sb, 1)

            shared_hidden(0)
            for t in range(NT):
                decay_scores(t, 0)
                decay_scores(t, 1)
                if t % CPB < CPB - 1:
                    decay_keys(t)
                if t >= 1:
                    normalise_output(t - 1)
                decay_scores(t, 2)
                decay_scores(t, 3)
                if t == T_RANK:
                    take_ranks()
                if t == T_INVERT:
                    take_inverse()
                if t == T_EXPERT:
                    take_block_experts()
                if t % CPB < CPB - 1:
                    update_state(t)
                if t + 1 < NT:
                    shared_hidden(t + 1)
                if t >= 1:
                    add_residual(t - 1)
                if t == T_RANK:
                    assign_slots()
                if t == T_RANK + 1:
                    one_hot_positions()
                if t == T_RANK + 2:
                    one_hot_blocks()
                if t == T_INVERT:
                    make_codes()
            normalise_output(NT - 1)

            def expert_step(q, u, i):
                n = RING * q + u
                if live(i, 0):
                    need(dve, tok_in[u], 16 * (q + 1))
                    nc.vector.tensor_copy(gidx[:, u:u + 1], codes[:, bass.ds(n + RING, 1), 0]).then_inc(gidx_sb, 1)
                if live(i, 1):
                    need(dve, sil_sb, n)
                    need(dve, eht_ps, n - 2)
                    nc.vector.tensor_tensor(eh[:, (u - 1) % 2, 0:I], sil[:, (u - 1) % 2, :],
                                            ps_gu[(u - 1) % 2][:, I:2 * I], ALU.mult).then_inc(eh_sb, 1)
                if live(i, 3):
                    w = (u - 3) % RING
                    need(dve, sent[w], 16 * (q + (u - 3) // RING))
                    nc.vector.tensor_copy(sidx[:, w:w + 1], codes[:, bass.ds(n - 3, 1), 1])
                    need(dve, dn_ps, n - 2)
                    nc.vector.tensor_copy(ysb[:, w, :], ps_dn[(u - 3) % 2][:, 0:D]).then_inc(ys_sb, 1)

            expert_loop(dve, expert_step, {2: lambda: add_residual(NT - 1)})

            for t in range(NT):
                dve.wait_ge(back_in[t], 16)
                for k in range(TOPK):
                    a = t * TOPK + k
                    ins = nc.vector.scalar_tensor_tensor(x_sb[:, t, :], back[:, t, k, :], rw[:, a:a + 1], x_sb[:, t, :],
                                                         ALU.mult, ALU.add)
                    if k < TOPK - 1:
                        step(ins)
                ins.then_inc(tot_sb, 1)

        @block.tensor
        def _(pe):
            pe.wait_ge(c_in, 48)
            for u in range(NT // 2):
                pe.wait_ge(xn_done, 2 * u + 2)
                if u >= 2:
                    pe.wait_ge(xnT_sb, u - 1)
                for g in range(KT):
                    for j in range(2):
                        o = (2 * g + j) * P
                        last = nc.tensor.transpose(ps_s[u % 2][:, o:o + P], xn[:, 2 * u + j, g * P:(g + 1) * P], ident)
                last.then_inc(xnT_ps, 1)
            for t in range(NT):
                if t % 2 == 0:
                    pe.wait_ge(xnT_sb, t // 2 + 1)
                for g in range(KT):
                    last = nc.tensor.matmul(ps_y[:, t * E:(t + 1) * E], xnT[:, g, t * P:(t + 1) * P], wr[:, g, :],
                                            start=(g == 0), stop=(g == KT - 1))
                last.then_inc(lg_ps, 1)

            def route_ranks():
                pe.wait_ge(pool_cst, 1)
                pe.wait_ge(mask_sb, 1)
                nc.tensor.matmul(ps_y[:, D:2 * D], lt_bf[:, :], mask[:, :, :].rearrange("p t e -> p (t e)"),
                                 start=True, stop=False, skip_group_check=True)
                for t in range(NT - 1):
                    after = NT - 1 - t
                    nc.tensor.matmul(ps_y[:, D + (t + 1) * E:2 * D].rearrange("p (t e) -> p t e", e=E), ones_bf[:, :],
                                     mask[:, t:t + 1, :].broadcast_to([P, after, E]),
                                     start=False, stop=True, skip_group_check=True)
                for t in range(NT):
                    last = nc.tensor.matmul(ps_y[:, 0:E], ones_bf[:, :], mask[:, t, :],
                                            start=False, stop=(t == NT - 1), skip_group_check=True)
                last.then_inc(rank_ps, 1)

            def route_inverse():
                pe.wait_ge(hot_sb, 1)
                for a in range(NA):
                    last = nc.tensor.matmul(ps_y[:, D:D + 2 * NB], pos_hot[:, a, :], blk_code[:, a, :],
                                            start=(a == 0), stop=(a == NA - 1))
                last.then_inc(inv_ps, 1)

            def tokens(g, t):
                return xnT[:, g, t * P:(t + 1) * P]

            def project_qk(t):
                if t >= 1:
                    pe.wait_ge(qk_sb, t)
                for m in range(2 * KT):
                    for g in range(KT):
                        last = nc.tensor.matmul(ps_qk[:, m * P:(m + 1) * P], wqkvg[:, g, m * P:(m + 1) * P],
                                                tokens(g, t), start=(g == 0), stop=(g == KT - 1))
                last.then_inc(qk_ps, 1)

            def project_vg(t):
                if t >= 1:
                    pe.wait_ge(vg_sb, 2 * t)
                for g in range(KT):
                    last = nc.tensor.matmul(ps_vg[:, :], tokens(g, t), wqkvg[:, g, 2 * D:4 * D],
                                            start=(g == 0), stop=(g == KT - 1))
                last.then_inc(vg_ps, 1)

            def project_shared(t):
                if t >= 1:
                    pe.wait_ge(hs_sb, t)
                for g in range(KT):
                    last = nc.tensor.matmul(ps_sg[:, 0:2 * I], tokens(g, t), wsgu[:, g, :],
                                            start=(g == 0), stop=(g == KT - 1))
                last.then_inc(sg_ps, 1)

            def scores(t, r):
                n = 4 * t + r
                if r == 0:
                    pe.wait_ge(q_ready, 3 * (t + 1))
                if n >= 2:
                    pe.wait_ge(sc_sb, n - 1)
                rows = slice(32 * r, 32 * (r + 1))
                for par, q in enumerate((qe, qo)):
                    for g in range(KT):
                        o = (2 * par + g) * P
                        last = nc.tensor.matmul(ps_s[r % 2][:, o:o + P],
                                                qk[rows, t % 2, (KT + g) * P:(KT + g + 1) * P],
                                                q[rows, t % 2, g * P:(g + 1) * P], start=True, stop=True)
                last.then_inc(sc_ps, 1)

            def transpose_keys(t):
                for g in range(KT):
                    last = nc.tensor.transpose(ps_tr[:, g * P:(g + 1) * P],
                                               qk[:, t % 2, (KT + g) * P:(KT + g + 1) * P], ident)
                last.then_inc(kt_ps, 1)

            def from_state(t):
                if t >= 1:
                    pe.wait_ge(yn_sb, t)
                else:
                    pe.wait_ge(mask_sb, 1)
                if t == T_RANK:
                    route_ranks()
                    pe.wait_ge(rank_sb, 1)
                if t == T_INVERT:
                    route_inverse()
                    pe.wait_ge(inv_sb, 1)
                if t == T_EXPERT:
                    pe.wait_ge(eid_in, 1)
                    nc.tensor.matmul(ps_y[0:1, D:D + NB], eid[:, :], ident[:, 0:NB], start=True, stop=True).then_inc(eid_ps, 1)
                    pe.wait_ge(eid_sb, 1)
                if t % CPB == 0:
                    return
                pe.wait_ge(st_sb, states_before(t))
                for g in range(KT):
                    nc.tensor.matmul(ps_y[:, g * P:(g + 1) * P], state[:, g * P:(g + 1) * P],
                                     qd[:, t % 2, g * P:(g + 1) * P], start=(g == 0), stop=False, skip_group_check=True)

            def chunk_products(t):
                pe.wait_ge(kt_sb, states_before(t) + 1)
                pe.wait_ge(vg_sb, 2 * (t + 1))
                if t >= 2:
                    pe.wait_ge(res_sb, t - 1)
                for g in range(KT):
                    last = nc.tensor.matmul(ps_po[:, g * P:(g + 1) * P], ktok[:, g * P:(g + 1) * P],
                                            v[:, t % 2, g * P:(g + 1) * P], start=True, stop=True)
                last.then_inc(pr_ps, 1)

            def weigh_values(t, r):
                pe.wait_ge(sc_sb, 4 * t + r + 1)
                if r == 0:
                    pe.wait_ge(vz_sb, t + 1)
                for s in range(4 * r, 4 * r + 4):
                    g, h = divmod(head_of_slot(s), HG)
                    last = nc.tensor.matmul(ps_y[:, g * P:(g + 1) * P], vz[:, g * VG + h * P:g * VG + (h + 1) * P],
                                            st[:, s * P:(s + 1) * P],
                                            start=(s == 0 and t % CPB == 0), stop=(s == H - 1), skip_group_check=True)
                if r == 3:
                    last.then_inc(y_ps, 1)

            def transpose_outputs(t):
                pe.wait_ge(yt_sb, t + 1)
                for g in range(KT):
                    last = nc.tensor.transpose(ps_y[:, D + g * P:D + (g + 1) * P], yT[:, g * P:(g + 1) * P], ident)
                last.then_inc(yt_ps, 1)

            def transpose_back(t):
                pe.wait_ge(hs_sb, t + 1)
                pe.wait_ge(z_sb, t + 1)
                nc.tensor.transpose(ps_tr[:, 0:P], hs[:, t % 2, 0:P], ident)
                nc.tensor.transpose(ps_tr[0:I2, P:2 * P], hs[:, t % 2, P:I], ident)
                for g in range(KT):
                    last = nc.tensor.transpose(ps_tr[:, (2 + g) * P:(3 + g) * P], z[:, t % 2, g * P:(g + 1) * P], ident)
                last.then_inc(trb_ps, 1)

            def project_out(t):
                pe.wait_ge(trb_sb, 3 * (t + 1))
                if t == 0:
                    pe.wait_ge(w_in, 80)
                pe.wait_ge(st_sb, states_before(min(t + 2, NT)))
                if t >= 1:
                    pe.wait_ge(res_sb, t)
                o = ps_po[:, D:2 * D]
                for g in range(KT):
                    nc.tensor.matmul(o, zT[:, g * P:(g + 1) * P], wo[:, g, :], start=(g == 0), stop=False)
                nc.tensor.matmul(o, hT1[:, :], wsd1[:, :], start=False, stop=False)
                nc.tensor.matmul(o, hT2[:, :], wsd2[:, :], start=False, stop=True).then_inc(o_ps, 1)

            pe.wait_ge(wq_in, 32)
            project_qk(0)
            project_vg(0)
            project_shared(0)
            for t in range(NT):
                more = t + 1 < NT
                scores(t, 0)
                scores(t, 1)
                if t >= 1:
                    transpose_outputs(t - 1)
                if t % CPB < CPB - 1:
                    transpose_keys(t)
                if more:
                    project_qk(t + 1)
                scores(t, 2)
                scores(t, 3)
                if more:
                    project_vg(t + 1)
                from_state(t)
                if t % CPB < CPB - 1:
                    chunk_products(t)
                weigh_values(t, 0)
                weigh_values(t, 1)
                if t >= 1:
                    if t % CPB < CPB - 1:
                        pe.wait_ge(kt_sb, states_before(t) + 1)
                    transpose_back(t - 1)
                if more:
                    project_shared(t + 1)
                weigh_values(t, 2)
                weigh_values(t, 3)
                if t >= 1:
                    project_out(t - 1)

            def finish_first_phase():
                transpose_back(NT - 1)
                project_out(NT - 1)

            def step(q, u, i):
                n = RING * q + u
                if live(i, 0):
                    need(pe, tok_in[u], 16 * (q + 1))
                    need(pe, xt_sb, n - 1)
                    for g in range(KT):
                        last = nc.tensor.transpose(ps_xt[u % 2][:, g * P:(g + 1) * P], xg[:, u, g * P:(g + 1) * P], ident)
                    last.then_inc(xt_ps, 1)
                if live(i, 1):
                    if i == 1:
                        pe.wait_ge(we_in, 16 * (LATE // 5 + 1))
                    e = expert(n - 1)
                    need(pe, xt_sb, n)
                    need(pe, eh_sb, n - 2)
                    for g in range(KT):
                        last = nc.tensor.matmul(ps_gu[(u - 1) % 2][:, 0:2 * I], xbT[:, (u - 1) % 2, g * P:(g + 1) * P],
                                                w1[:, bass.ds(e * EW + g * 2 * I, 2 * I)],
                                                start=(g == 0), stop=(g == KT - 1))
                    last.then_inc(gu_ps, 1)
                if live(i, 2):
                    need(pe, eh_sb, n - 1)
                    need(pe, eht_sb, n - 3)
                    for g, f in enumerate((0, I2)):
                        last = nc.tensor.transpose(ps_eht[u % 2][:, g * P:(g + 1) * P], eh[:, u % 2, f:f + P], ident)
                    last.then_inc(eht_ps, 1)
                if live(i, 3):
                    e = expert(n - 3)
                    need(pe, eht_sb, n - 2)
                    need(pe, ys_sb, n - 4)
                    nc.tensor.matmul(ps_dn[(u - 3) % 2][:, 0:D], ehT[:, (u - 3) % 2, P:2 * P],
                                     w1[:, bass.ds(e * EW + KT * 2 * I, D)], start=True, stop=False)
                    nc.tensor.matmul(ps_dn[(u - 3) % 2][:, 0:D], ehT[0:I2, (u - 3) % 2, 0:P],
                                     w2[0:I2, bass.ds(e * D, D)], start=False, stop=True).then_inc(dn_ps, 1)

            def expert(b):
                return pe.value_load(eid_row[0:1, bass.ds(b, 1)], min_val=0, max_val=E - 1)

            def wait_late():
                pe.wait_ge(wl_in[0], 16 * ((E - LATE) // 2 + 1))
                pe.wait_ge(wl_in[1], 16 * ((E - LATE + 1) // 2))

            expert_loop(pe, step, {0: lambda: transpose_outputs(NT - 1), 2: finish_first_phase,
                                   3: lambda: pe.wait_ge(res_sb, NT)}, wait_late)


def expert_weights(a):
    gu = np.concatenate([a["ffn_gate_w"], a["ffn_up_w"]], axis=1).transpose(2, 0, 1)
    gu = gu.reshape(KT, P, E, 2 * I).transpose(1, 2, 0, 3).reshape(P, E, KT * 2 * I)
    down = a["ffn_down_w"][:, :, I2:].transpose(2, 0, 1)
    return np.ascontiguousarray(np.concatenate([gu, down], axis=2)).reshape(P, E * EW)


def kernel(**inp):
    import concourse.bacc as bacc
    from concourse.bass_utils import run_bass_kernel_spmd

    a = {k[3:]: np.asarray(v) for k, v in inp.items()}

    def by_rows(w):
        return np.ascontiguousarray(w.reshape(-1, P, w.shape[1]).transpose(1, 0, 2))

    consts, decay = constants()
    arrays = {
        "x": a["attn_x"],
        "consts": consts,
        "decay": decay,
        "w_router": by_rows(a["ffn_router_w"].T),
        "w_qkvg": by_rows(np.concatenate([a["attn_w" + n].T for n in "qkvg"], axis=1)),
        "w_out": by_rows(a["attn_wo"].T),
        "w_sgu": by_rows(np.concatenate([a["ffn_shared_gate_w"].T, a["ffn_shared_up_w"].T], axis=1)),
        "w_sd1": np.ascontiguousarray(a["ffn_shared_down_w"].T[:P]),
        "w_sd2": np.ascontiguousarray(a["ffn_shared_down_w"].T[P:]),
        "lnwb": np.stack([a["attn_ln_w"], a["attn_ln_b"]]),
        "rbias": a["ffn_router_b"],
        "w_exp": expert_weights(a),
        "w_exp2": np.ascontiguousarray(a["ffn_down_w"][:, :, :I2].transpose(2, 0, 1)).reshape(I2, E * D),
    }
    nc = bacc.Bacc("TRN2", target_bir_lowering=False, num_devices=1)
    args = [nc.dram_tensor(n + "_dram", v.shape, F32, kind="ExternalInput").ap() for n, v in arrays.items()]
    out = nc.dram_tensor("out_dram", (BATCH, SEQ, D), F32, kind="ExternalOutput").ap()
    xn_rows = nc.dram_tensor("xn_rows", (TOK, D), F32, kind="Internal").ap()
    y_rows = nc.dram_tensor("y_rows", (ROWS, D), F32, kind="Internal").ap()
    build(nc, *args, xn_rows, y_rows, out)
    r = run_bass_kernel_spmd(nc, [{n + "_dram": v for n, v in arrays.items()}], core_ids=[0])
    return r.results[0]["out_dram"]
```

```python
from contextlib import ExitStack

import numpy as np

import concourse.bass as bass
from concourse import mybir

F32 = mybir.dt.float32
BF16 = mybir.dt.bfloat16
U32 = mybir.dt.uint32
I32 = mybir.dt.int32
ALU = mybir.AluOpType
ACT = mybir.ActivationFunctionType
AX_X = mybir.AxisListType.X

P = 128
BATCH, SEQ, D = 2, 512, 256
TOK = BATCH * SEQ
NT = TOK // P
CPB = SEQ // P
KT = D // P
H, HD = 16, 16
HG = P // HD
SCALE = HD ** -0.5
EPS = 1e-5
E, TOPK, I = 32, 4, 192
I2 = I - P
RSCALE = 1.8
RSQRT_MAGIC = 0x5F3759DF
EW = KT * 2 * I + D
ROWS = TOK * TOPK
RING = 4
NB = -(-(E + (ROWS - 1) // P) // RING) * RING
FEWEST = E // RING
STRIDE = 4
LAST_MIXED = 4
MAXB = TOK // P
NA = NT * TOPK
LATE = 15
Q_FIRST = 2
Q_LATE = (LATE + 1) // RING
Q_END = NB // RING
T_RANK, T_INVERT, T_EXPERT = 1, 4, 5
DVE_PARTS, POOL_TILES = (((1, 0, D), (2, 0, D)), ((4, 0, D), (5, 0, D)), ((7, 0, D // 2), (7, D // 2, D))), (0, 3, 6)
TOTAL_ORDER = (1, 2, 0, 4, 5, 3, 6, 7)
WARM_UP = 16
LAG = 7

C_ID = 0
C_BM = C_ID + P
C_QD = C_BM + P
C_KD = C_QD + KT * P
C_GC = C_KD + H
C_PM = C_GC + KT
C_IO = C_PM + 2
C_PI = C_IO + P
C_FILL = C_PI + 1
C_TK = C_FILL + 1
C_LT = C_TK + NA
C_END = C_LT + P


def head_of_slot(s):
    r, par, g = s // 4, s // 2 % 2, s % 2
    return HG * g + 2 * r + par


def constants():
    gammas = (1.0 - np.exp(np.linspace(np.log(1 / 32), np.log(1 / 64), H)).astype(np.float32)).astype(np.float64)
    i = np.arange(P)
    c = np.zeros((P, C_END))
    c[:, C_ID:C_ID + P] = np.eye(P)
    c[:, C_BM:C_BM + P] = i[:, None] // HD == i[None, :] // HD
    for g in range(KT):
        row_gamma = gammas[HG * g + i // HD]
        c[:, C_QD + g * P:C_QD + (g + 1) * P] = SCALE * row_gamma[:, None] ** (i[None, :] + 1)
        c[:, C_GC + g] = row_gamma ** P
    c[:, C_KD:C_KD + H] = gammas[None, :] ** (P - 1 - i[:, None])
    for par in range(2):
        c[:, C_PM + par] = i // HD % 2 == par
    c[:, C_IO:C_IO + P] = i[None, :]
    c[:, C_PI] = i
    c[:, C_FILL] = ROWS + P + i
    for t in range(NT):
        for k in range(TOPK):
            c[:, C_TK + t * TOPK + k] = 1 + k * NT + t
    c[:, C_LT:C_LT + P] = i[:, None] < i[None, :]
    dist = i[None, :] - i[:, None]
    decay = np.zeros((P, H, P))
    for s in range(H):
        decay[:, s] = np.where(dist >= 0, SCALE * gammas[head_of_slot(s)] ** np.maximum(dist, 0), 0.0)
    return c.astype(np.float32), decay.reshape(P, H * P).astype(np.float32)


def build(nc, x, consts, decay, w_router, w_qkvg, w_out, w_sgu, w_sd1, w_sd2, lnwb, rbias, w_exp, w_exp2, xn_rows, y_rows, out):
    with ExitStack() as ctx:
        def sb(name, shape, dt=F32):
            return ctx.enter_context(nc.sbuf_tensor(name, shape, dt))

        def sem(name):
            return ctx.enter_context(nc.semaphore(name))

        w1 = sb("w1", [P, E * EW])
        w2 = sb("w2", [P, E * D])
        free1, free2 = [LATE * EW], [LATE * D]

        def early(*shape, dt=F32, of=w1, free=free1):
            n = int(np.prod(shape)) * mybir.dt.size(dt) // 4
            ap = of[:, free[0]:free[0] + n]
            free[0] += n
            assert free[0] <= of.shape[1]
            if dt != F32:
                ap = ap.bitcast(dt)
            if len(shape) == 2:
                ap = ap.rearrange("p (a b) -> p a b", a=shape[0])
            return ap

        x_sb = sb("x_sb", [P, NT, D])
        cst = sb("cst", [P, C_END])
        rw = sb("rw", [P, NA])
        codes = sb("codes", [P, NB + RING, 2], U32)
        eid_row = sb("eid_row", [1, NB + 1], I32)

        VG = HG * (P + HD)
        vz = early(KT * VG)
        xn = vz[:, 0:NT * D].rearrange("p (t d) -> p t d", t=NT)
        xnT = early(KT, TOK)
        dec = early(H * P)
        wqkvg = early(KT, 4 * D)
        st = early(H * P)
        wo = early(KT, D)
        wsgu = early(KT, 2 * I)
        wsd1 = early(D)
        lnw = early(D)
        lnb = early(D)
        wr = early(KT, E)
        rb = early(E)
        qk = early(2, 4 * P)
        qe = early(2, KT * P)
        qo = early(2, KT * P)
        qd = early(2, KT * P)
        v = early(2, D)
        wsd2 = sb("wsd2", [I2, D])
        stats = sb("stats", [P, NT, 6])
        mv = sb("mv", [P, NT, 2])
        rstd = sb("rstd", [P, NT])
        var = sb("var", [P, NT])
        newton = sb("newton", [P, NT])
        half_v = sb("half_v", [P, NT])
        gate = early(3, D)
        ktok = sb("ktok", [P, D])
        state_mem = sb("state_mem", [P, 2 * KT * P])
        state = state_mem[:, 0:KT * P]
        pmask = state_mem[:, KT * P:2 * KT * P]
        ystats = sb("ystats", [P, 6])
        ymv = sb("ymv", [P, 2])
        yrstd = sb("yrstd", [P, 1])
        yn = sb("yn", [P, 2, D])
        z1 = sb("z1", [P, D])
        z = early(2, D)
        sgs = sb("sgs", [P, I])
        hs = sb("hs", [P, 2, I])
        yT = sb("yT", [P, KT * P])
        zT = sb("zT", [P, KT * P])
        hT1 = sb("hT1", [P, P])
        hT2 = sb("hT2", [I2, P])

        logits = sb("logits", [P, NT, E])
        top = sb("top", [P, NT, 8])
        topi = sb("topi", [P, NT, 8], U32)
        topf = sb("topf", [P, NT, TOPK])
        ex = sb("ex", [P, NT, TOPK])
        exs = sb("exs", [P, NT])
        chosen = sb("chosen", [P, NA, E], BF16)
        mask = sb("mask", [P, NT, E], BF16)
        lt_bf = sb("lt_bf", [P, P], BF16)
        ones_bf = sb("ones_bf", [P, P], BF16)
        ranks = sb("ranks", [P, NT, E])
        counts = sb("counts", [P, E])
        over = sb("over", [P, E, MAXB - 1], BF16)
        nblk = sb("nblk", [P, E])
        ends = sb("ends", [P, E])
        ones_e = sb("ones_e", [P, E])
        base = sb("base", [P, E])
        slot_k = sb("slot_k", [P, NA])
        slot_i = sb("slot_i", [P, NA], U32)
        blk_i = sb("blk_i", [P, NA], U32)
        pos_i = sb("pos_i", [P, NA], U32)
        blk_f = sb("blk_f", [P, NA])
        pos_f = sb("pos_f", [P, NA])
        prod = early(NA, E, of=w2, free=free2)
        pos_hot = early(NA, P, dt=BF16, of=w2, free=free2)
        blk_hot = early(NA, NB, dt=BF16, of=w2, free=free2)
        loop_mem = sb("loop_mem", [P, RING * D + 2 * KT * P + 2 * I + 2 * NB])
        blk_code = loop_mem[:, 0:NA * NB].bitcast(BF16).rearrange("p (a b) -> p a b", a=NA)

        xg = sb("xg", [P, RING, D])
        xbT = sb("xbT", [P, 2, KT * P])
        eh = state_mem[:, 0:2 * I].rearrange("p (a b) -> p a b", a=2)
        gidx = sb("gidx", [P, RING], U32)
        sidx = sb("sidx", [P, RING], U32)
        ysb = loop_mem[:, 0:RING * D].rearrange("p (a b) -> p a b", a=RING)
        ehT = loop_mem[:, RING * D:RING * D + 2 * KT * P].rearrange("p (a b) -> p a b", a=2)
        sil = loop_mem[:, RING * D + 2 * KT * P:RING * D + 2 * KT * P + 2 * I].rearrange("p (a b) -> p a b", a=2)
        back = w1[:, 0:NA * D].rearrange("p (t k d) -> p t k d", t=NT, k=TOPK)
        inv = sb("inv", [P, 2 * NB])
        unused = sb("unused", [P, NB])
        code_f = sb("code_f", [P, NB])
        le = sb("le", [P, E])
        rounds_i = sb("rounds_i", [1, 1], I32)
        eid = sb("eid", [P, 1])

        bank = [ctx.enter_context(nc.psum_tensor(f"bank{i}", [P, 512], F32)) for i in range(8)]
        ps_tr, ps_qk, ps_vg, ps_sg, ps_s0, ps_s1, ps_y, ps_po = bank
        ps_s = [ps_s0, ps_s1]
        ps_xt, ps_gu, ps_eht, ps_dn = [ps_qk, ps_vg], [ps_sg, ps_s0], [ps_s1, ps_tr], [ps_po, ps_y]

        ident = cst[:, C_ID:C_ID + P]

        x_in = [sem(f"x_in{i}") for i in range(NT // 2)]
        c_in = sem("c_in")
        r_in = sem("r_in")
        w_in = sem("w_in")
        wqk_in = sem("wqk_in")
        wvg_in = sem("wvg_in")
        wsg_in = sem("wsg_in")
        d_in = sem("d_in")
        dve_step = sem("dve_step")
        pool_seq = sem("pool_seq")
        xn_done = sem("xn_done")
        xnT_ps = sem("xnT_ps")
        xnT_sb = sem("xnT_sb")
        lg_ps = sem("lg_ps")
        lg_sb = sem("lg_sb")
        qk_ps = sem("qk_ps")
        qk_sb = sem("qk_sb")
        q_ready = sem("q_ready")
        vz_sb = sem("vz_sb")
        yt_sb = sem("yt_sb")
        yt_ps = sem("yt_ps")
        vg_ps = sem("vg_ps")
        vg_sb = sem("vg_sb")
        sg_ps = sem("sg_ps")
        sgs_sb = sem("sgs_sb")
        hs_sb = sem("hs_sb")
        sc_ps = sem("sc_ps")
        sc_sb = sem("sc_sb")
        kt_ps = sem("kt_ps")
        kt_sb = sem("kt_sb")
        pr_ps = sem("pr_ps")
        st_sb = sem("st_sb")
        y_ps = sem("y_ps")
        yn_sb = sem("yn_sb")
        z_sb = sem("z_sb")
        trb_ps = sem("trb_ps")
        trb_sb = sem("trb_sb")
        o_ps = sem("o_ps")
        res_sb = sem("res_sb")
        out_done = sem("out_done")
        xn_out = sem("xn_out")
        we_in = sem("we_in")
        wl_in = [sem(f"wl_in{i}") for i in range(2)]
        ones_sb = sem("ones_sb")
        pool_cst = sem("pool_cst")
        soft_in = sem("soft_in")
        soft_ex = sem("soft_ex")
        mask_sb = sem("mask_sb")
        rank_ps = sem("rank_ps")
        rank_sb = sem("rank_sb")
        hot_sb = sem("hot_sb")
        inv_ps = sem("inv_ps")
        inv_sb = sem("inv_sb")
        eid_ps = sem("eid_ps")
        eid_in = sem("eid_in")
        eid_sb = sem("eid_sb")
        gidx_sb = sem("gidx_sb")
        pool_go = sem("pool_go")
        tok_in = [sem(f"tok_in{i}") for i in range(RING)]
        xt_ps = sem("xt_ps")
        xt_sb = sem("xt_sb")
        gu_ps = sem("gu_ps")
        sil_sb = sem("sil_sb")
        eh_sb = sem("eh_sb")
        eht_ps = sem("eht_ps")
        eht_sb = sem("eht_sb")
        dn_ps = sem("dn_ps")
        ys_sb = sem("ys_sb")
        sent = [sem(f"sent{i}") for i in range(RING)]
        back_in = [sem(f"back_in{i}") for i in range(NT)]
        wtd_sb = sem("wtd_sb")
        tot_sb = [sem(f"tot_sb{i}") for i in range(NT)]

        block = ctx.enter_context(nc.Block())
        x_v = x.rearrange("b (t p) d -> p (b t) d", p=P)
        out_v = out.rearrange("b (t p) d -> p (b t) d", p=P)

        def states_before(t):
            return sum(1 for u in range(t) if u % CPB < CPB - 1)

        def need(eng, semaphore, value):
            if not isinstance(value, int) or value > 0:
                eng.wait_ge(semaphore, value)

        def filled_rounds(eng):
            eng.wait_ge(eid_sb, 1)
            return FEWEST + eng.value_load(eid_row[0:1, NB:NB + 1], min_val=0, max_val=Q_END - FEWEST)

        def expert_loop(eng, step, first, finish_first_phase, await_late=None):
            for i in range(first, RING * Q_FIRST):
                step(i // RING, i % RING, i)
                if i == LAST_MIXED:
                    finish_first_phase()
            with eng.Fori(Q_FIRST, Q_LATE) as q:
                for u in range(RING):
                    step(q, u, None)
            with eng.Fori(Q_LATE, FEWEST, 2) as q2:
                for q in (q2, q2 + 1):
                    if await_late:
                        await_late(q)
                    for u in range(RING):
                        step(q, u, None)
            rounds = filled_rounds(eng)
            for start in range(FEWEST, Q_END, STRIDE):
                with eng.If(rounds > start):
                    with eng.Fori(start, start + STRIDE) as q:
                        with eng.If(q < rounds):
                            for u in range(RING):
                                step(q, u, None)
            for u in range(3):
                step(rounds, u, NB + u)

        def live(i, stage):
            return i is None or 0 <= i - stage < NB

        @block.sync
        def _(sp):
            for u in range(NT // 2):
                s = slice(2 * u, 2 * u + 2)
                sp.dma_start(x_sb[:, s, :], x_v[:, s, :]).then_inc(x_in[u], 16)
            sp.dma_start(wqkvg[:, :, 0:2 * D], w_qkvg[:, :, 0:2 * D]).then_inc(wqk_in, 16)
            sp.dma_start(wqkvg[:, :, 2 * D:4 * D], w_qkvg[:, :, 2 * D:4 * D]).then_inc(wvg_in, 16)
            sp.dma_start(wsgu[:, :, :], w_sgu).then_inc(wsg_in, 16)
            sp.dma_start(dec[:, :], decay).then_inc(d_in, 16)
            sp.dma_start(wo[:, :, :], w_out).then_inc(w_in, 16)
            sp.dma_start(wsd1[:, :], w_sd1).then_inc(w_in, 16)
            sp.dma_start(wsd2[:, :], w_sd2).then_inc(w_in, 16)
            sp.dma_start(lnw[:, :], lnwb[0].partition_broadcast(P)).then_inc(w_in, 16)
            sp.dma_start(lnb[:, :], lnwb[1].partition_broadcast(P)).then_inc(w_in, 16)
            for half in range(2):
                s = slice(half * NT // 2, (half + 1) * NT // 2)
                sp.wait_ge(xn_done, (half + 1) * NT // 2)
                sp.dma_start(xn_rows.rearrange("(t p) d -> p t d", p=P)[:, s, :], xn[:, s, :]).then_inc(xn_out, 16)
            for e in range(0, LATE, 5):
                sp.dma_start(w1[:, e * EW:(e + 5) * EW], w_exp[:, e * EW:(e + 5) * EW]).then_inc(we_in, 16)
            sp.dma_start(w2[0:I2, 0:LATE * D], w_exp2[:, 0:LATE * D]).then_inc(we_in, 16)
            sp.wait_ge(xn_out, 32)
            sp.wait_ge(res_sb, NT)
            sp.dma_start(w2[0:I2, LATE * D:E * D], w_exp2[:, LATE * D:E * D]).then_inc(wl_in[0], 16)
            for n, e in enumerate(range(LATE, E), 1):
                if n >= 2:
                    sp.wait_ge(wl_in[n % 2], 16 * (n // 2))
                sp.dma_start(w1[:, e * EW:(e + 1) * EW], w_exp[:, e * EW:(e + 1) * EW]).then_inc(wl_in[n % 2], 16)
            rounds = filled_rounds(sp)
            for s in range(RING):
                sp.wait_ge(sent[s], 16 * rounds)
            y_v = y_rows.rearrange("(k t p) d -> t p k d", t=NT, p=P)
            for t in range(NT):
                sp.dma_start(back[:, t], y_v[t]).then_inc(back_in[t], 16)
            for t in TOTAL_ORDER:
                sp.wait_ge(tot_sb[t], sum(n == t for pair in DVE_PARTS for n, _, _ in pair) + (t in POOL_TILES))
                sp.dma_start(out_v[:, t, :], x_sb[:, t, :]).then_inc(out_done, 16)
            sp.wait_ge(out_done, 16 * NT)

        @block.scalar
        def _(act):
            act.dma_start(cst[:, :], consts).then_inc(c_in, 16)
            act.wait_ge(ones_sb, 1)
            nc.scalar.activation(sgs[:, 0:1], ones_bf[:, 0:1], ACT.Silu)
            act.dma_start(wr[:, :, :], w_router).then_inc(r_in, 16)
            act.dma_start(rb[:, :], rbias.partition_broadcast(P)).then_inc(r_in, 16)

            def take_features(u):
                act.wait_ge(xnT_ps, u + 1)
                nc.scalar.copy(xnT[:, :, 2 * u * P:2 * (u + 1) * P],
                               ps_s[u % 2][:, :].rearrange("p (g n) -> p g n", g=KT)).then_inc(xnT_sb, 1)

            def take_projections(t):
                act.wait_ge(qk_ps, t + 1)
                nc.scalar.copy(qk[:, t % 2, :], ps_qk[:, :]).then_inc(qk_sb, 1)
                act.wait_ge(vg_ps, t + 1)
                nc.scalar.copy(v[:, t % 2, :], ps_vg[:, 0:D]).then_inc(vg_sb, 1)
                nc.scalar.activation(gate[:, t % 3, :], ps_vg[:, D:2 * D], ACT.Silu).then_inc(vg_sb, 1)

            def take_shared_gate(t):
                act.wait_ge(sg_ps, t + 1)
                nc.scalar.activation(sgs[:, :], ps_sg[:, 0:I], ACT.Silu).then_inc(sgs_sb, 1)

            def take_transposed(t):
                act.wait_ge(trb_ps, t + 1)
                nc.scalar.copy(hT1[:, :], ps_tr[:, 0:P]).then_inc(trb_sb, 1)
                nc.scalar.copy(hT2[:, :], ps_tr[0:I2, P:2 * P]).then_inc(trb_sb, 1)
                nc.scalar.copy(zT[:, :], ps_tr[:, 2 * P:4 * P]).then_inc(trb_sb, 1)

            def take_outputs(t):
                act.wait_ge(y_ps, t + 1)
                nc.scalar.copy(yT[:, :], ps_y[:, 0:D]).then_inc(yt_sb, 1)

            def step(q, u, i):
                n = RING * q + u
                if live(i, 0):
                    need(act, xt_ps, n + 1)
                    need(act, gu_ps, n - 1)
                    nc.scalar.copy(xbT[:, u % 2, :], ps_xt[u % 2][:, 0:KT * P]).then_inc(xt_sb, 1)
                if live(i, 1):
                    need(act, gu_ps, n)
                    need(act, eh_sb, n - 2)
                    nc.scalar.activation(sil[:, (u - 1) % 2, :], ps_gu[(u - 1) % 2][:, 0:I], ACT.Silu).then_inc(sil_sb, 1)
                if live(i, 2):
                    need(act, eht_ps, n - 1)
                    need(act, dn_ps, n - 3)
                    nc.scalar.copy(ehT[:, u % 2, :], ps_eht[u % 2][:, 0:KT * P]).then_inc(eht_sb, 1)

            take_features(0)
            take_projections(0)
            take_shared_gate(0)
            for u in range(1, NT // 2):
                take_features(u)
            for t in range(NT):
                if t + 1 < NT:
                    take_projections(t + 1)
                if t == NT - 1:
                    step(0, 0, 0)
                    step(0, 1, 1)
                if t >= 1:
                    take_transposed(t - 1)
                if t + 1 < NT:
                    take_shared_gate(t + 1)
                if t == 0:
                    act.wait_ge(soft_in, 1)
                    nc.scalar.activation(ex[:, :, :], ex[:, :, :], ACT.Exp).then_inc(soft_ex, 1)
                take_outputs(t)

            expert_loop(act, step, 2, lambda: take_transposed(NT - 1))

            for n in POOL_TILES:
                act.wait_ge(back_in[n], 16)
                for k in range(TOPK):
                    a = n * TOPK + k
                    nc.scalar.activation(back[:, n, k, :], back[:, n, k, :], ACT.Copy,
                                         scale=rw[:, a:a + 1]).then_inc(wtd_sb, 1)

        @block.gpsimd
        def _(pool):
            steps = [0]

            def step(ins):
                steps[0] += 1
                ins.then_inc(pool_seq, 1)
                pool.wait_ge(pool_seq, steps[0])

            def mask_queries(t):
                pool.wait_ge(qk_sb, t + 1)
                if t == 0:
                    pool.wait_ge(c_in, 16)
                q = qk[:, t % 2, 0:KT * P]
                nc.gpsimd.tensor_scalar(qe[:, t % 2, :], q, cst[:, C_PM:C_PM + 1], None, ALU.mult).then_inc(q_ready, 1)
                nc.gpsimd.tensor_scalar(qo[:, t % 2, :], q, cst[:, C_PM + 1:C_PM + 2], None, ALU.mult).then_inc(q_ready, 1)
                nc.gpsimd.tensor_tensor(qd[:, t % 2, :], q, cst[:, C_QD:C_QD + KT * P], ALU.mult).then_inc(q_ready, 1)

            def gate_output(t):
                pool.wait_ge(yn_sb, t + 1)
                if t == 0:
                    pool.wait_ge(w_in, 80)
                step(nc.gpsimd.tensor_tensor(z1[:, :], yn[:, t % 2, :], lnw[:, :], ALU.mult))
                step(nc.gpsimd.tensor_tensor(z1[:, :], z1[:, :], lnb[:, :], ALU.add))
                pool.wait_ge(vg_sb, 2 * (t + 1))
                nc.gpsimd.tensor_tensor(z[:, t % 2, :], z1[:, :], gate[:, t % 3, :], ALU.mult).then_inc(z_sb, 1)

            def pool_step(q, u, j):
                n = RING * q + u
                if live(j, 0):
                    need(pool, gidx_sb, n + 1)
                    pool.sem_inc(pool_go, 1)
                    need(pool, xt_ps, n - RING + 1)
                    pool.sem_inc(pool_go, 1)
                    nc.gpsimd.indirect_dma_start(
                        xg[:, u, :], None, xn_rows, bass.IndirectOffsetOnAxis(ap=gidx[:, u:u + 1], axis=0),
                    ).then_inc(tok_in[u], 16)
                if live(j, LAG):
                    w = (u - LAG) % RING
                    need(pool, ys_sb, n - LAG + 1)
                    pool.sem_inc(pool_go, 1)
                    nc.gpsimd.indirect_dma_start(
                        y_rows, bass.IndirectOffsetOnAxis(ap=sidx[:, w:w + 1], axis=0), ysb[:, w, :], None,
                        bounds_check=ROWS - 1, oob_is_err=False,
                    ).then_inc(sent[w], 16)

            def spread_values(t):
                pool.wait_ge(vg_sb, 2 * (t + 1))
                if t >= 1:
                    pool.wait_ge(y_ps, t)
                nc.gpsimd.tensor_copy(vz[:, :].rearrange("p (h c) -> p h c", c=P + HD)[:, :, 0:HD],
                                      v[:, t % 2, :].rearrange("p (h d) -> p h d", d=HD)).then_inc(vz_sb, 1)

            nc.gpsimd.memset(ones_bf[:, :], 1.0).then_inc(ones_sb, 1)
            pool.wait_ge(c_in, 16)
            nc.gpsimd.memset(ones_e[:, :], 1.0)
            nc.gpsimd.tensor_copy(lt_bf[:, :], cst[:, C_LT:C_LT + P]).then_inc(pool_cst, 1)
            mask_queries(0)
            pool.wait_ge(xn_out, 32)
            pool.wait_ge(xnT_ps, NT // 2)
            step(nc.gpsimd.memset(vz[:, :], 0.0))
            for t in range(NT):
                spread_values(t)
                if t + 1 < NT:
                    mask_queries(t + 1)
                if t >= 1:
                    gate_output(t - 1)
                if t == T_EXPERT:
                    for j in range(RING):
                        pool_step(0, j, j)
            for j in range(RING, Q_FIRST * RING):
                if j == LAST_MIXED + 2:
                    gate_output(NT - 1)
                pool_step(j // RING, j % RING, j)
            rounds = filled_rounds(pool)
            with pool.Fori(Q_FIRST, Q_END) as q:
                with pool.If(q < rounds):
                    for u in range(RING):
                        pool_step(q, u, None)
            for j in range(LAG):
                pool_step(rounds + j // RING, j % RING, NB + j)

            pool.wait_ge(res_sb, NT)
            for i, n in enumerate(POOL_TILES):
                for k in range(TOPK):
                    pool.wait_ge(wtd_sb, TOPK * i + k + 1)
                    ins = nc.gpsimd.tensor_tensor(x_sb[:, n, :], x_sb[:, n, :], back[:, n, k, :], ALU.add)
                    if k < TOPK - 1:
                        step(ins)
                    else:
                        ins.then_inc(tot_sb[n], 1)

        @block.vector
        def _(dve):
            steps = [0]

            def step(ins):
                steps[0] += 1
                ins.then_inc(dve_step, 1)
                dve.wait_ge(dve_step, steps[0])

            def inverse_sqrt(y, variance, v, a, h, between=()):
                fill = iter(between)

                def link(ins):
                    steps[0] += 1
                    ins.then_inc(dve_step, 1)
                    next(fill, lambda: None)()
                    dve.wait_ge(dve_step, steps[0])

                nc.vector.tensor_scalar(h, variance, EPS, -0.5, ALU.add, ALU.mult)
                link(nc.vector.tensor_scalar(v, variance, EPS, None, ALU.add))
                link(nc.vector.tensor_scalar(a.bitcast(I32), v.bitcast(I32), 1, None, ALU.logical_shift_right))
                link(nc.vector.tensor_scalar(y.bitcast(I32), a.bitcast(I32), -1, RSQRT_MAGIC, ALU.mult, ALU.add))
                for _ in range(3):
                    if y.shape[-1] == 1:
                        link(nc.vector.scalar_tensor_tensor(a, y, y, h, ALU.mult, ALU.mult))
                    else:
                        link(nc.vector.tensor_tensor(a, y, y, ALU.mult))
                        link(nc.vector.tensor_tensor(a, a, h, ALU.mult))
                    link(nc.vector.scalar_tensor_tensor(y, a, 1.5, y, ALU.add, ALU.mult))
                for f in fill:
                    f()

            def moments(t):
                if t % 2 == 0:
                    dve.wait_ge(x_in[t // 2], 16)
                return nc.vector.bn_stats(stats[:, t, :], x_sb[:, t, :])

            def aggregate(t):
                return nc.vector.bn_aggr(mv[:, t, :], stats[:, t, :])

            def normalise(t):
                nc.vector.tensor_scalar(xn[:, t, :], x_sb[:, t, :], mv[:, t, 0:1], rstd[:, t:t + 1],
                                        ALU.subtract, ALU.mult).then_inc(xn_done, 1)

            dve.wait_ge(x_in[0], 16)
            moments(0)
            step(moments(1))
            aggregate(0)
            step(aggregate(1))
            inverse_sqrt(rstd[:, 0:2], mv[:, 0:2, 1], var[:, 0:2], newton[:, 0:2], half_v[:, 0:2],
                         [lambda: None] * 4 + [lambda: moments(2), lambda: moments(3)])
            normalise(0)
            normalise(1)
            for t in range(4, NT):
                last = moments(t)
            step(last)
            for t in range(2, NT):
                last = aggregate(t)
            step(last)
            inverse_sqrt(rstd[:, 2:NT], mv[:, 2:NT, 1], var[:, 2:NT], newton[:, 2:NT], half_v[:, 2:NT])
            for t in range(2, NT):
                normalise(t)

            def take_logits():
                dve.wait_ge(lg_ps, NT)
                dve.wait_ge(r_in, 32)
                ins = nc.vector.tensor_tensor(logits[:, :, :], ps_po[:, 0:NT * E].rearrange("p (t e) -> p t e", t=NT),
                                              rb[:, :].unsqueeze(1).broadcast_to([P, NT, E]), ALU.add)
                ins.then_inc(lg_sb, 1)

            def choose_experts():
                dve.wait_ge(lg_sb, 1)
                for t in range(NT):
                    last = nc.vector.max(top[:, t, :], logits[:, t, :])
                step(last)
                for t in range(NT):
                    last = nc.vector.max_index(topi[:, t, :], top[:, t, :], logits[:, t, :])
                step(last)
                nc.vector.tensor_tensor(ex[:, :, :], top[:, :, 0:TOPK], top[:, :, 0:1].broadcast_to([P, NT, TOPK]),
                                        ALU.subtract).then_inc(soft_in, 1)
                step(nc.vector.tensor_copy(topf[:, :, :], topi[:, :, 0:TOPK]))
                step(nc.vector.tensor_tensor(
                    chosen[:, :, :], cst[:, C_IO:C_IO + E].unsqueeze(1).broadcast_to([P, NA, E]),
                    topf[:, :, :].rearrange("p t k -> p (t k)").unsqueeze(2).broadcast_to([P, NA, E]), ALU.is_equal))
                with nc.allow_low_precision(reason="the sums are 0 or 1"):
                    nc.vector.tensor_reduce(mask[:, :, :], chosen[:, :, :].rearrange("p (t k) e -> p t e k", k=TOPK),
                                            AX_X, ALU.add).then_inc(mask_sb, 1)

            def weigh_choices():
                dve.wait_ge(soft_ex, 1)
                step(nc.vector.reduce_sum(exs[:, :], ex[:, :, :], AX_X))
                step(nc.vector.reciprocal(exs[:, :], exs[:, :]))
                nc.vector.scalar_tensor_tensor(rw[:, :].rearrange("p (t k) -> p t k", k=TOPK), ex[:, :, :], RSCALE,
                                               exs[:, :].unsqueeze(2).broadcast_to([P, NT, TOPK]), ALU.mult, ALU.mult)

            def take_ranks():
                dve.wait_ge(rank_ps, 1)
                nc.vector.tensor_copy(ranks[:, :, :], ps_y[:, D:2 * D].rearrange("p (t e) -> p t e", t=NT))
                nc.vector.tensor_scalar(counts[:, :], ps_y[:, 0:E], 1.0 / P, None, ALU.mult).then_inc(rank_sb, 1)

            def assign_slots():
                dve.wait_ge(rank_sb, 1)
                step(nc.vector.tensor_tensor(over[:, :, :], counts[:, :].unsqueeze(2).broadcast_to([P, E, MAXB - 1]),
                                             cst[:, C_IO + 1:C_IO + MAXB].unsqueeze(1).broadcast_to([P, E, MAXB - 1]),
                                             ALU.is_gt))
                step(nc.vector.reduce_sum(nblk[:, :], over[:, :, :], AX_X))
                step(nc.vector.tensor_scalar(nblk[:, :], nblk[:, :], 1.0, None, ALU.add))
                dve.wait_ge(pool_cst, 1)
                step(nc.vector.tensor_tensor_scan(ends[:, :], ones_e[:, :], nblk[:, :], 0.0, ALU.mult, ALU.add))
                step(nc.vector.tensor_tensor(base[:, :], ends[:, :], nblk[:, :], ALU.subtract))
                step(nc.vector.tensor_scalar(base[:, :], base[:, :], float(P), None, ALU.mult))
                step(nc.vector.tensor_tensor(ranks[:, :, :], ranks[:, :, :],
                                             base[:, :].unsqueeze(1).broadcast_to([P, NT, E]), ALU.add))
                step(nc.vector.tensor_tensor(
                    prod[:, :, :].rearrange("p (t k) e -> p t k e", k=TOPK),
                    chosen[:, :, :].rearrange("p (t k) e -> p t k e", k=TOPK),
                    ranks[:, :, :].unsqueeze(2).broadcast_to([P, NT, TOPK, E]), ALU.mult))
                step(nc.vector.reduce_sum(slot_k[:, :], prod[:, :, :], AX_X))
                step(nc.vector.tensor_copy(slot_i[:, :], slot_k[:, :]))
                step(nc.vector.tensor_scalar(blk_i[:, :], slot_i[:, :], P.bit_length() - 1, None,
                                             ALU.logical_shift_right))
                step(nc.vector.tensor_scalar(pos_i[:, :], slot_i[:, :], P - 1, None, ALU.bitwise_and))
                nc.vector.tensor_copy(blk_f[:, :], blk_i[:, :])
                step(nc.vector.tensor_copy(pos_f[:, :], pos_i[:, :]))

            def one_hot_positions():
                nc.vector.tensor_tensor(pos_hot[:, :, :], cst[:, C_IO:C_IO + P].unsqueeze(1).broadcast_to([P, NA, P]),
                                        pos_f[:, :].unsqueeze(2).broadcast_to([P, NA, P]), ALU.is_equal)

            def one_hot_blocks():
                step(nc.vector.tensor_tensor(blk_hot[:, :, :], cst[:, C_IO:C_IO + NB].unsqueeze(1).broadcast_to([P, NA, NB]),
                                             blk_f[:, :].unsqueeze(2).broadcast_to([P, NA, NB]), ALU.is_equal))
                nc.vector.tensor_tensor(blk_code[:, :, 0:NB], blk_hot[:, :, :],
                                        cst[:, C_TK:C_TK + NA].unsqueeze(2).broadcast_to([P, NA, NB]), ALU.mult)
                nc.vector.tensor_scalar(blk_code[:, :, NB:2 * NB], blk_hot[:, :, :], cst[:, C_PI:C_PI + 1], None,
                                        ALU.mult).then_inc(hot_sb, 1)

            def take_inverse():
                dve.wait_ge(inv_ps, 1)
                nc.vector.tensor_copy(inv[:, :], ps_y[:, D:D + 2 * NB]).then_inc(inv_sb, 1)

            def make_codes():
                dve.wait_ge(inv_sb, 1)
                nc.vector.tensor_scalar(unused[:, :], inv[:, 0:NB], 0.0, cst[:, C_FILL:C_FILL + 1],
                                        ALU.is_equal, ALU.mult)
                nc.vector.memset(codes[:, NB:NB + RING, :], 0)
                step(nc.vector.tensor_scalar(code_f[:, :], inv[:, 0:NB], float(P), float(-P), ALU.mult, ALU.add))
                step(nc.vector.tensor_tensor(code_f[:, :], code_f[:, :], unused[:, :], ALU.add))
                step(nc.vector.tensor_tensor(codes[:, 0:NB, 1], code_f[:, :], inv[:, NB:2 * NB], ALU.add))
                step(nc.vector.tensor_scalar(codes[:, 0:NB, 0], codes[:, 0:NB, 1], TOK - 1, None, ALU.bitwise_and))
                nc.vector.tensor_copy(gidx[:, :], codes[:, 0:RING, 0]).then_inc(gidx_sb, RING)
                step(nc.vector.tensor_scalar(rounds_i[:, :], ends[0:1, E - 1:E], float(RING - 1 - E), None, ALU.add))
                nc.vector.tensor_scalar(eid_row[:, NB:NB + 1], rounds_i[:, :], RING.bit_length() - 1, None,
                                        ALU.logical_shift_right)
                step(nc.vector.tensor_scalar(le[:, :], ends[:, :], cst[:, C_PI:C_PI + 1], None, ALU.is_le))
                step(nc.vector.reduce_sum(eid[:, :], le[:, :], AX_X))
                nc.vector.tensor_scalar(eid[:, :], eid[:, :], float(E - 1), None, ALU.min).then_inc(eid_in, 1)

            def take_block_experts():
                dve.wait_ge(eid_ps, 1)
                nc.vector.tensor_copy(eid_row[:, 0:NB], ps_y[0:1, D:D + NB]).then_inc(eid_sb, 1)

            def decay_scores(t, r):
                dve.wait_ge(sc_ps, 4 * t + r + 1)
                if t == 0 and r == 0:
                    dve.wait_ge(d_in, 16)
                nc.vector.tensor_tensor(st[:, 4 * r * P:4 * (r + 1) * P], ps_s[r % 2][:, :],
                                        dec[:, 4 * r * P:4 * (r + 1) * P], ALU.mult).then_inc(sc_sb, 1)

            def decay_keys(t):
                dve.wait_ge(kt_ps, states_before(t) + 1)
                nc.vector.tensor_tensor(ktok[:, :].rearrange("p (h d) -> p h d", h=H),
                                        ps_tr[:, 0:D].rearrange("p (h d) -> p h d", h=H),
                                        cst[:, C_KD:C_KD + H].unsqueeze(2).broadcast_to([P, H, HD]),
                                        ALU.mult).then_inc(kt_sb, 1)

            def update_state(t):
                dve.wait_ge(pr_ps, states_before(t) + 1)
                first = t % CPB == 0
                to = state if first else pmask
                ins = nc.vector.tensor_tensor(to[:, :].rearrange("p (g n) -> p g n", g=KT),
                                              ps_po[:, 0:KT * P].rearrange("p (g n) -> p g n", g=KT),
                                              cst[:, C_BM:C_BM + P].unsqueeze(1).broadcast_to([P, KT, P]), ALU.mult)
                if first:
                    ins.then_inc(st_sb, 1)
                    return
                step(ins)
                for g in range(KT):
                    s = slice(g * P, (g + 1) * P)
                    last = nc.vector.scalar_tensor_tensor(state[:, s], state[:, s], cst[:, C_GC + g:C_GC + g + 1],
                                                          pmask[:, s], ALU.mult, ALU.add)
                last.then_inc(st_sb, 1)

            def shared_hidden(t):
                dve.wait_ge(sgs_sb, t + 1)
                nc.vector.tensor_tensor(hs[:, t % 2, :], sgs[:, :], ps_sg[:, I:2 * I], ALU.mult).then_inc(hs_sb, 1)

            def add_residual(t):
                dve.wait_ge(o_ps, t + 1)
                nc.vector.tensor_tensor(x_sb[:, t, :], x_sb[:, t, :], ps_po[:, D:2 * D], ALU.add).then_inc(res_sb, 1)

            def normalise_output(t, between=()):
                dve.wait_ge(yt_ps, t + 1)
                step(nc.vector.bn_stats(ystats[:, :], ps_y[:, D:2 * D]))
                step(nc.vector.bn_aggr(ymv[:, :], ystats[:, :]))
                inverse_sqrt(yrstd[:, :], ymv[:, 1:2], var[:, 0:1], newton[:, 0:1], half_v[:, 0:1], between)
                if t >= 2:
                    dve.wait_ge(z_sb, t - 1)
                nc.vector.tensor_scalar(yn[:, t % 2, :], ps_y[:, D:2 * D], ymv[:, 0:1], yrstd[:, :],
                                        ALU.subtract, ALU.mult).then_inc(yn_sb, 1)

            def expert_step(q, u, i):
                n = RING * q + u
                if live(i, 0):
                    need(dve, tok_in[u], 16 * (q + 1))
                    nc.vector.tensor_copy(gidx[:, u:u + 1], codes[:, bass.ds(n + RING, 1), 0]).then_inc(gidx_sb, 1)
                if live(i, 1):
                    need(dve, sil_sb, n)
                    need(dve, eht_ps, n - 2)
                    nc.vector.tensor_tensor(eh[:, (u - 1) % 2, 0:I], sil[:, (u - 1) % 2, :],
                                            ps_gu[(u - 1) % 2][:, I:2 * I], ALU.mult).then_inc(eh_sb, 1)
                if live(i, 3):
                    w = (u - 3) % RING
                    need(dve, sent[w], 16 * (q + (u - 3) // RING))
                    nc.vector.tensor_copy(sidx[:, w:w + 1], codes[:, bass.ds(n - 3, 1), 1])
                    need(dve, dn_ps, n - 2)
                    nc.vector.tensor_copy(ysb[:, w, :], ps_dn[(u - 3) % 2][:, 0:D]).then_inc(ys_sb, 1)

            shared_hidden(0)
            for t in range(NT):
                decay_scores(t, 0)
                decay_scores(t, 1)
                if t % CPB < CPB - 1:
                    decay_keys(t)
                if t == 0:
                    take_logits()
                if t >= 1:
                    normalise_output(t - 1)
                decay_scores(t, 2)
                decay_scores(t, 3)
                if t == NT - 1:
                    expert_step(0, 0, 0)
                if t == T_RANK:
                    take_ranks()
                if t == T_INVERT:
                    take_inverse()
                if t == T_EXPERT:
                    take_block_experts()
                if t == 0:
                    choose_experts()
                if t % CPB < CPB - 1:
                    update_state(t)
                if t == T_RANK:
                    assign_slots()
                if t == T_RANK + 1:
                    one_hot_positions()
                if t == T_RANK + 2:
                    one_hot_blocks()
                if t + 1 < NT:
                    shared_hidden(t + 1)
                if t == T_RANK:
                    weigh_choices()
                if t == T_INVERT:
                    make_codes()
                if t >= 1:
                    add_residual(t - 1)
            dve.wait_ge(y_ps, NT)
            expert_step(0, 1, 1)
            normalise_output(NT - 1, [lambda: None] * 7 + [lambda: expert_step(0, 2, 2)])

            expert_loop(dve, expert_step, 3, lambda: add_residual(NT - 1))

            for pair in DVE_PARTS:
                done = {}
                for k in range(TOPK):
                    for n, lo, hi in pair:
                        if k == 0:
                            dve.wait_ge(back_in[n], 16)
                        else:
                            dve.wait_ge(dve_step, done[n, lo])
                        a = n * TOPK + k
                        ins = nc.vector.scalar_tensor_tensor(x_sb[:, n, lo:hi], back[:, n, k, lo:hi], rw[:, a:a + 1],
                                                             x_sb[:, n, lo:hi], ALU.mult, ALU.add)
                        if k < TOPK - 1:
                            steps[0] += 1
                            done[n, lo] = steps[0]
                            ins.then_inc(dve_step, 1)
                        else:
                            ins.then_inc(tot_sb[n], 1)

        @block.tensor
        def _(pe):
            def warm_up(n):
                for _ in range(n):
                    nc.tensor.matmul(ps_y[:, :], ones_bf[:, :], ones_bf[:, :].unsqueeze(1).broadcast_to([P, 4, P]),
                                     start=True, stop=True)

            pe.wait_ge(ones_sb, 1)
            warm_up(WARM_UP)
            pe.wait_ge(c_in, 16)

            def transpose_tokens(u):
                pe.wait_ge(xn_done, 2 * u + 2)
                if u >= 2:
                    pe.wait_ge(xnT_sb, u - 1)
                for g in range(KT):
                    for j in range(2):
                        o = (2 * g + j) * P
                        last = nc.tensor.transpose(ps_s[u % 2][:, o:o + P], xn[:, 2 * u + j, g * P:(g + 1) * P], ident)
                last.then_inc(xnT_ps, 1)

            def router_logits(t):
                if t == 0:
                    pe.wait_ge(r_in, 32)
                if t % 2 == 0:
                    pe.wait_ge(xnT_sb, t // 2 + 1)
                for g in range(KT):
                    last = nc.tensor.matmul(ps_po[:, t * E:(t + 1) * E], xnT[:, g, t * P:(t + 1) * P], wr[:, g, :],
                                            start=(g == 0), stop=(g == KT - 1))
                last.then_inc(lg_ps, 1)

            def route_ranks():
                pe.wait_ge(pool_cst, 1)
                pe.wait_ge(mask_sb, 1)
                nc.tensor.matmul(ps_y[:, D:2 * D], lt_bf[:, :], mask[:, :, :].rearrange("p t e -> p (t e)"),
                                 start=True, stop=False, skip_group_check=True)
                for t in range(NT - 1):
                    after = NT - 1 - t
                    nc.tensor.matmul(ps_y[:, D + (t + 1) * E:2 * D].rearrange("p (t e) -> p t e", e=E), ones_bf[:, :],
                                     mask[:, t:t + 1, :].broadcast_to([P, after, E]),
                                     start=False, stop=True, skip_group_check=True)
                for t in range(NT):
                    last = nc.tensor.matmul(ps_y[:, 0:E], ones_bf[:, :], mask[:, t, :],
                                            start=False, stop=(t == NT - 1), skip_group_check=True)
                last.then_inc(rank_ps, 1)

            def route_inverse():
                pe.wait_ge(hot_sb, 1)
                for a in range(NA):
                    last = nc.tensor.matmul(ps_y[:, D:D + 2 * NB], pos_hot[:, a, :], blk_code[:, a, :],
                                            start=(a == 0), stop=(a == NA - 1))
                last.then_inc(inv_ps, 1)

            def tokens(g, t):
                return xnT[:, g, t * P:(t + 1) * P]

            def project_qk(t, between=lambda m: None):
                if t >= 1:
                    pe.wait_ge(qk_sb, t)
                for m in range(2 * KT):
                    between(m)
                    for g in range(KT):
                        last = nc.tensor.matmul(ps_qk[:, m * P:(m + 1) * P], wqkvg[:, g, m * P:(m + 1) * P],
                                                tokens(g, t), start=(g == 0), stop=(g == KT - 1))
                last.then_inc(qk_ps, 1)

            def project_vg(t):
                if t >= 1:
                    pe.wait_ge(vg_sb, 2 * t)
                for g in range(KT):
                    last = nc.tensor.matmul(ps_vg[:, :], tokens(g, t), wqkvg[:, g, 2 * D:4 * D],
                                            start=(g == 0), stop=(g == KT - 1))
                last.then_inc(vg_ps, 1)

            def project_shared(t):
                if t >= 1:
                    pe.wait_ge(hs_sb, t)
                for g in range(KT):
                    last = nc.tensor.matmul(ps_sg[:, 0:2 * I], tokens(g, t), wsgu[:, g, :],
                                            start=(g == 0), stop=(g == KT - 1))
                last.then_inc(sg_ps, 1)

            def scores(t, half):
                if half == 0:
                    pe.wait_ge(q_ready, 3 * (t + 1))
                if t + half > 0:
                    pe.wait_ge(sc_sb, 4 * t + 2 * half)
                for par, q in enumerate((qe, qo)):
                    for g in range(KT):
                        for b in range(2):
                            rows = slice(32 * (2 * half + b), 32 * (2 * half + b + 1))
                            o = (2 * par + g) * P
                            last = nc.tensor.matmul(ps_s[b][:, o:o + P],
                                                    qk[rows, t % 2, (KT + g) * P:(KT + g + 1) * P],
                                                    q[rows, t % 2, g * P:(g + 1) * P], start=True, stop=True)
                            if par == 1 and g == KT - 1:
                                last.then_inc(sc_ps, 1)

            def transpose_keys(t):
                for g in range(KT):
                    last = nc.tensor.transpose(ps_tr[:, g * P:(g + 1) * P],
                                               qk[:, t % 2, (KT + g) * P:(KT + g + 1) * P], ident)
                last.then_inc(kt_ps, 1)

            def route(t):
                if t >= 1:
                    pe.wait_ge(yn_sb, t)
                if t == T_RANK:
                    route_ranks()
                if t == T_INVERT:
                    route_inverse()
                if t == T_EXPERT:
                    pe.wait_ge(eid_in, 1)
                    nc.tensor.matmul(ps_y[0:1, D:D + NB], eid[:, :], ident[:, 0:NB], start=True, stop=True).then_inc(eid_ps, 1)

            def from_state(t):
                if t == T_RANK:
                    pe.wait_ge(rank_sb, 1)
                if t == T_INVERT:
                    pe.wait_ge(inv_sb, 1)
                if t == T_EXPERT:
                    pe.wait_ge(eid_sb, 1)
                if t % CPB == 0:
                    return
                pe.wait_ge(st_sb, states_before(t))
                for g in range(KT):
                    last = nc.tensor.matmul(ps_y[:, g * P:(g + 1) * P], state[:, g * P:(g + 1) * P],
                                            qd[:, t % 2, g * P:(g + 1) * P], start=(g == 0), stop=False, skip_group_check=True)
                if t % CPB < CPB - 1:
                    last.then_inc(pr_ps, 1)

            def chunk_products(t):
                pe.wait_ge(kt_sb, states_before(t) + 1)
                pe.wait_ge(vg_sb, 2 * (t + 1))
                if t == 0:
                    pe.wait_ge(lg_sb, 1)
                if t >= 2:
                    pe.wait_ge(res_sb, t - 1)
                for g in range(KT):
                    last = nc.tensor.matmul(ps_po[:, g * P:(g + 1) * P], ktok[:, g * P:(g + 1) * P],
                                            v[:, t % 2, g * P:(g + 1) * P], start=True, stop=True)
                if t % CPB == 0:
                    last.then_inc(pr_ps, 1)

            def weigh_values(t, r):
                pe.wait_ge(sc_sb, 4 * t + r + 1)
                if r == 0:
                    pe.wait_ge(vz_sb, t + 1)
                for s in range(4 * r, 4 * r + 4):
                    g, h = divmod(head_of_slot(s), HG)
                    last = nc.tensor.matmul(ps_y[:, g * P:(g + 1) * P], vz[:, g * VG + h * P:g * VG + (h + 1) * P],
                                            st[:, s * P:(s + 1) * P],
                                            start=(s == 0 and t % CPB == 0), stop=(s == H - 1), skip_group_check=True)
                if r == 3:
                    last.then_inc(y_ps, 1)

            def transpose_outputs(t):
                pe.wait_ge(yt_sb, t + 1)
                for g in range(KT):
                    last = nc.tensor.transpose(ps_y[:, D + g * P:D + (g + 1) * P], yT[:, g * P:(g + 1) * P], ident)
                last.then_inc(yt_ps, 1)

            def transpose_back(t):
                pe.wait_ge(hs_sb, t + 1)
                pe.wait_ge(z_sb, t + 1)
                nc.tensor.transpose(ps_tr[:, 0:P], hs[:, t % 2, 0:P], ident)
                nc.tensor.transpose(ps_tr[0:I2, P:2 * P], hs[:, t % 2, P:I], ident)
                for g in range(KT):
                    last = nc.tensor.transpose(ps_tr[:, (2 + g) * P:(3 + g) * P], z[:, t % 2, g * P:(g + 1) * P], ident)
                last.then_inc(trb_ps, 1)

            def project_out(t):
                pe.wait_ge(trb_sb, 3 * t + 1)
                if t == 0:
                    pe.wait_ge(w_in, 80)
                pe.wait_ge(st_sb, states_before(min(t + 2, NT)))
                if t >= 1:
                    pe.wait_ge(res_sb, t)
                o = ps_po[:, D:2 * D]
                nc.tensor.matmul(o, hT1[:, :], wsd1[:, :], start=True, stop=False)
                pe.wait_ge(trb_sb, 3 * t + 2)
                nc.tensor.matmul(o, hT2[:, :], wsd2[:, :], start=False, stop=False)
                pe.wait_ge(trb_sb, 3 * t + 3)
                for g in range(KT):
                    last = nc.tensor.matmul(o, zT[:, g * P:(g + 1) * P], wo[:, g, :], start=False, stop=(g == KT - 1))
                last.then_inc(o_ps, 1)

            def finish_first_phase():
                pe.wait_ge(eht_sb, LAST_MIXED - 2)
                transpose_back(NT - 1)
                pe.wait_ge(ys_sb, 1)
                project_out(NT - 1)

            def step(q, u, i):
                n = RING * q + u
                if live(i, 1):
                    e_gu = expert(n - 1)
                if live(i, 3):
                    e_dn = expert(n - 3)
                if live(i, 0):
                    need(pe, tok_in[u], 16 * (q + 1))
                    need(pe, xt_sb, n - 1)
                    for g in range(KT):
                        last = nc.tensor.transpose(ps_xt[u % 2][:, g * P:(g + 1) * P], xg[:, u, g * P:(g + 1) * P], ident)
                    last.then_inc(xt_ps, 1)
                if live(i, 1):
                    if i == 1:
                        pe.wait_ge(we_in, 16 * (LATE // 5 + 1))
                    need(pe, xt_sb, n)
                    need(pe, eh_sb, n - 2)
                    for g in range(KT):
                        last = nc.tensor.matmul(ps_gu[(u - 1) % 2][:, 0:2 * I], xbT[:, (u - 1) % 2, g * P:(g + 1) * P],
                                                w1[:, bass.ds(e_gu * EW + g * 2 * I, 2 * I)],
                                                start=(g == 0), stop=(g == KT - 1))
                    last.then_inc(gu_ps, 1)
                if live(i, 2):
                    need(pe, eh_sb, n - 1)
                    need(pe, eht_sb, n - 3)
                    for g, f in enumerate((0, I2)):
                        last = nc.tensor.transpose(ps_eht[u % 2][:, g * P:(g + 1) * P], eh[:, u % 2, f:f + P], ident)
                    last.then_inc(eht_ps, 1)
                if live(i, 3):
                    need(pe, eht_sb, n - 2)
                    need(pe, ys_sb, n - 4)
                    if i == 3:
                        pe.wait_ge(res_sb, NT - 1)
                    if i == 4:
                        pe.wait_ge(yn_sb, NT)
                    if i == LAST_MIXED + 1:
                        pe.wait_ge(res_sb, NT)
                    nc.tensor.matmul(ps_dn[(u - 3) % 2][:, 0:D], ehT[:, (u - 3) % 2, P:2 * P],
                                     w1[:, bass.ds(e_dn * EW + KT * 2 * I, D)], start=True, stop=False)
                    nc.tensor.matmul(ps_dn[(u - 3) % 2][:, 0:D], ehT[0:I2, (u - 3) % 2, 0:P],
                                     w2[0:I2, bass.ds(e_dn * D, D)], start=False, stop=True).then_inc(dn_ps, 1)

            def expert(b):
                return pe.value_load(eid_row[0:1, bass.ds(b, 1)], min_val=0, max_val=E - 1)

            def await_late(q):
                for late in wl_in:
                    pe.wait_ge(late, 16 * (RING // 2 * (q + 1) - (LATE - 1) // 2))

            transpose_tokens(0)
            warm_up(WARM_UP // 4)
            pe.wait_ge(xnT_sb, 1)
            pe.wait_ge(wqk_in, 16)
            project_qk(0)
            pe.wait_ge(wvg_in, 16)
            project_vg(0)
            pe.wait_ge(wsg_in, 16)
            project_shared(0)
            for u in range(1, NT // 2):
                transpose_tokens(u)
            def some_logits(m):
                for t in range(m * NT // 4, (m + 1) * NT // 4):
                    router_logits(t)

            project_qk(1, some_logits)
            for t in range(NT):
                more = t + 1 < NT
                scores(t, 0)
                if t >= 1:
                    transpose_outputs(t - 1)
                if t % CPB < CPB - 1:
                    transpose_keys(t)
                if t == 0:
                    project_vg(1)
                elif more:
                    project_qk(t + 1)
                else:
                    pe.wait_ge(vg_sb, 2 * NT)
                    pe.wait_ge(hs_sb, NT)
                    step(0, 0, 0)
                    step(0, 1, 1)
                scores(t, 1)
                if t >= 1 and more:
                    project_vg(t + 1)
                route(t)
                if t % CPB < CPB - 1:
                    chunk_products(t)
                from_state(t)
                weigh_values(t, 0)
                weigh_values(t, 1)
                if t >= 1:
                    if t % CPB < CPB - 1:
                        pe.wait_ge(kt_sb, states_before(t) + 1)
                    transpose_back(t - 1)
                if more:
                    project_shared(t + 1)
                weigh_values(t, 2)
                weigh_values(t, 3)
                if t >= 1:
                    project_out(t - 1)

            transpose_outputs(NT - 1)
            expert_loop(pe, step, 2, finish_first_phase, await_late)


def expert_weights(a):
    gu = np.concatenate([a["ffn_gate_w"], a["ffn_up_w"]], axis=1).transpose(2, 0, 1)
    gu = gu.reshape(KT, P, E, 2 * I).transpose(1, 2, 0, 3).reshape(P, E, KT * 2 * I)
    down = a["ffn_down_w"][:, :, I2:].transpose(2, 0, 1)
    return np.ascontiguousarray(np.concatenate([gu, down], axis=2)).reshape(P, E * EW)


def kernel(**inp):
    import concourse.bacc as bacc
    from concourse.bass_utils import run_bass_kernel_spmd

    a = {k[3:]: np.asarray(v) for k, v in inp.items()}

    def by_rows(w):
        return np.ascontiguousarray(w.reshape(-1, P, w.shape[1]).transpose(1, 0, 2))

    consts, decay = constants()
    arrays = {
        "x": a["attn_x"],
        "consts": consts,
        "decay": decay,
        "w_router": by_rows(a["ffn_router_w"].T),
        "w_qkvg": by_rows(np.concatenate([a["attn_w" + n].T for n in "qkvg"], axis=1)),
        "w_out": by_rows(a["attn_wo"].T),
        "w_sgu": by_rows(np.concatenate([a["ffn_shared_gate_w"].T, a["ffn_shared_up_w"].T], axis=1)),
        "w_sd1": np.ascontiguousarray(a["ffn_shared_down_w"].T[:P]),
        "w_sd2": np.ascontiguousarray(a["ffn_shared_down_w"].T[P:]),
        "lnwb": np.stack([a["attn_ln_w"], a["attn_ln_b"]]),
        "rbias": a["ffn_router_b"],
        "w_exp": expert_weights(a),
        "w_exp2": np.ascontiguousarray(a["ffn_down_w"][:, :, :I2].transpose(2, 0, 1)).reshape(I2, E * D),
    }
    nc = bacc.Bacc("TRN2", target_bir_lowering=False, num_devices=1)
    args = [nc.dram_tensor(n + "_dram", v.shape, F32, kind="ExternalInput").ap() for n, v in arrays.items()]
    out = nc.dram_tensor("out_dram", (BATCH, SEQ, D), F32, kind="ExternalOutput").ap()
    xn_rows = nc.dram_tensor("xn_rows", (TOK, D), F32, kind="Internal").ap()
    y_rows = nc.dram_tensor("y_rows", (ROWS, D), F32, kind="Internal").ap()
    build(nc, *args, xn_rows, y_rows, out)
    r = run_bass_kernel_spmd(nc, [{n + "_dram": v for n, v in arrays.items()}], core_ids=[0])
    return r.results[0]["out_dram"]
```
